# Optimizing a Trainium2 kernel written in Bass

```python
import numpy as np
import jax
import jax.numpy as jnp

def _softmax(x, axis=-1):
    return jax.nn.softmax(x, axis=axis)

def _gelu(x):
    return jax.nn.gelu(x, approximate=True)

def _silu(x):
    return jax.nn.silu(x)

def _sigmoid(x):
    return jax.nn.sigmoid(x)

def _layernorm(x, axis=-1, eps=1e-05):
    m = jnp.mean(x, axis=axis, keepdims=True)
    v = jnp.var(x, axis=axis, keepdims=True)
    return (x - m) / jnp.sqrt(v + eps)

def _scatter_add(tgt, idx, src, axis=0):
    return tgt.at[idx].add(src)

def _segment_sum(src, seg, n):
    return jax.ops.segment_sum(src, seg, n)
kernel_name = 'mk_flamingo_gated_d1_seqx_r8_929d22'

def setup_inputs(seed: int=0):
    np.random.seed(seed)
    _w = jnp.asarray

    def _rec_inputs():
        import jax
        import jax.numpy as jnp
        _rk = jax.random.key(seed)
        x = 0.0002417 + 0.9998 * jax.random.normal(jax.random.fold_in(_rk, 1), (8, 128, 128), jnp.float32)
        _lenS = 128 - jax.random.randint(jax.random.fold_in(_rk, 7), (8,), 0, max(1, 128 // 4) + 1, jnp.int32)
        _lenS2 = 128 - jax.random.randint(jax.random.fold_in(_rk, 8), (8,), 0, max(1, 128 // 4) + 1, jnp.int32)
        _ctx_1024P = jax.random.normal(jax.random.fold_in(_rk, 11), (8, 16, 128), jnp.float32)
        _ctx_1024c = jax.random.dirichlet(jax.random.fold_in(_rk, 511), 0.3 * jnp.ones((16,), jnp.float32), (8, 128))
        _ctx_1024t = jnp.einsum('bsk,bkd->bsd', _ctx_1024c, _ctx_1024P)
        _ctx_1024t = _ctx_1024t * jax.lax.rsqrt(jnp.mean(jnp.square(_ctx_1024t)) + 1e-12) * 0.953939
        ctx_1024 = 7.22013e-05 + 1.00017 * (_ctx_1024t + 0.3 * jax.random.normal(jax.random.fold_in(_rk, 611), (8, 128, 128), jnp.float32))
        _g = jax.random.normal(jax.random.fold_in(_rk, 9001), (2, 1), jnp.float32)
        _g = jnp.sign(_g) * jnp.maximum(jnp.abs(_g), 1.0) + (_g == 0) * 1.0
        g_xattn = _g[0]
        g_ffn = _g[1]
        return (x, ctx_1024, g_xattn, g_ffn)
    x, ctx_1024, g_xattn, g_ffn = _rec_inputs()

    def _L0_xattn_setup():
        import jax, jax.numpy as jnp
        import numpy as np
        D_MODEL = 128
        B, S = (4, 256)
        key = jax.random.key(seed)
        ks = jax.random.split(key, 10)
        s = 1.0 / np.sqrt(D_MODEL)
        return {'k': jax.random.normal(ks[0], (B, S, D_MODEL), jnp.float32), 'v': jax.random.normal(ks[1], (B, S, D_MODEL), jnp.float32), 'q': jax.random.normal(ks[2], (B, S, D_MODEL), jnp.float32), 'Wk': jax.random.normal(ks[3], (D_MODEL, D_MODEL), jnp.float32) * s, 'Wv': jax.random.normal(ks[4], (D_MODEL, D_MODEL), jnp.float32) * s, 'bv': jnp.zeros((D_MODEL,), jnp.float32), 'Wq': jax.random.normal(ks[5], (D_MODEL, D_MODEL), jnp.float32) * s, 'bq': jnp.zeros((D_MODEL,), jnp.float32), 'Wo': jax.random.normal(ks[6], (D_MODEL, D_MODEL), jnp.float32) * s, 'bo': jnp.zeros((D_MODEL,), jnp.float32)}
    _L0_xattn_all = _L0_xattn_setup()
    _L0_xattn_in = {k: v for k, v in _L0_xattn_all.items() if k in ('Wk', 'Wv', 'bv', 'Wq', 'bq', 'Wo', 'bo')}
    del _L0_xattn_all

    def _L0_ffn_setup():
        import jax, jax.numpy as jnp
        import numpy as np
        B, S, D = (4, 512, 128)
        H = 512
        RH = 128
        E = 16
        K = 2
        NS = 1

        def _swiglu(x, w1, w2, w3):
            return jax.nn.silu(x @ w1) * (x @ w2) @ w3
        key = jax.random.key(seed)
        ks = jax.random.split(key, 9)
        s = 0.02
        return {'x': jax.random.normal(ks[0], (B, S, D), dtype=jnp.float32), 'router_w': jax.random.normal(ks[1], (D, E), dtype=jnp.float32) * s, 'expert_bias': jnp.zeros((E,), dtype=jnp.float32), 'shared_w1': jax.random.normal(ks[2], (NS, D, H), dtype=jnp.float32) * s, 'shared_w2': jax.random.normal(ks[3], (NS, D, H), dtype=jnp.float32) * s, 'shared_w3': jax.random.normal(ks[4], (NS, H, D), dtype=jnp.float32) * s, 'routed_w1': jax.random.normal(ks[5], (E, D, RH), dtype=jnp.float32) * s, 'routed_w2': jax.random.normal(ks[6], (E, D, RH), dtype=jnp.float32) * s, 'routed_w3': jax.random.normal(ks[7], (E, RH, D), dtype=jnp.float32) * s}
    _L0_ffn_all = _L0_ffn_setup()
    _L0_ffn_in = {k: v for k, v in _L0_ffn_all.items() if k in ('router_w', 'expert_bias', 'shared_w1', 'shared_w2', 'shared_w3', 'routed_w1', 'routed_w2', 'routed_w3')}
    del _L0_ffn_all
    return {'x': x, 'ctx_1024': ctx_1024, 'g_xattn': g_xattn, 'g_ffn': g_ffn, 'L0_xattn_Wk': _L0_xattn_in['Wk'], 'L0_xattn_Wv': _L0_xattn_in['Wv'], 'L0_xattn_bv': _L0_xattn_in['bv'], 'L0_xattn_Wq': _L0_xattn_in['Wq'], 'L0_xattn_bq': _L0_xattn_in['bq'], 'L0_xattn_Wo': _L0_xattn_in['Wo'], 'L0_xattn_bo': _L0_xattn_in['bo'], 'L0_ffn_router_w': _L0_ffn_in['router_w'], 'L0_ffn_expert_bias': _L0_ffn_in['expert_bias'], 'L0_ffn_shared_w1': _L0_ffn_in['shared_w1'], 'L0_ffn_shared_w2': _L0_ffn_in['shared_w2'], 'L0_ffn_shared_w3': _L0_ffn_in['shared_w3'], 'L0_ffn_routed_w1': _L0_ffn_in['routed_w1'], 'L0_ffn_routed_w2': _L0_ffn_in['routed_w2'], 'L0_ffn_routed_w3': _L0_ffn_in['routed_w3']}

def reference(x, ctx_1024, g_xattn, g_ffn, L0_xattn_Wk, L0_xattn_Wv, L0_xattn_bv, L0_xattn_Wq, L0_xattn_bq, L0_xattn_Wo, L0_xattn_bo, L0_ffn_router_w, L0_ffn_expert_bias, L0_ffn_shared_w1, L0_ffn_shared_w2, L0_ffn_shared_w3, L0_ffn_routed_w1, L0_ffn_routed_w2, L0_ffn_routed_w3):
    import jax
    import jax.numpy as jnp

    def _L0_xattn_ref(k, v, q, Wk, Wv, bv, Wq, bq, Wo, bo):
        import jax, jax.numpy as jnp
        import numpy as np
        D_MODEL = 128
        B, S = (4, 256)
        kp = jnp.einsum('bsd,ed->bse', k, Wk)
        vp = jnp.einsum('bsd,ed->bse', v, Wv) + bv
        qp = jnp.einsum('bsd,ed->bse', q, Wq) + bq
        scale = 1.0 / jnp.sqrt(jnp.float32(kp.shape[-1]))
        scores = jnp.einsum('bqd,bkd->bqk', qp, kp) * scale
        probs = jax.nn.softmax(scores, axis=-1)
        ctx = jnp.einsum('bqk,bkd->bqd', probs, vp)
        return jnp.einsum('bqd,ed->bqe', ctx, Wo) + bo

    def _L0_ffn_ref(x, router_w, expert_bias, shared_w1, shared_w2, shared_w3, routed_w1, routed_w2, routed_w3):
        import jax, jax.numpy as jnp
        import numpy as np
        B, S, D = (4, 512, 128)
        H = 512
        RH = 128
        E = 16
        K = 2
        NS = 1

        def _swiglu(x, w1, w2, w3):
            return jax.nn.silu(x @ w1) * (x @ w2) @ w3
        shared_out = jnp.sum(jax.vmap(lambda w1, w2, w3: _swiglu(x, w1, w2, w3))(shared_w1, shared_w2, shared_w3), axis=0)
        scores = jax.nn.sigmoid(x @ router_w)
        sel_scores = scores + expert_bias
        _, top_idx = jax.lax.top_k(sel_scores, K)
        top_scores = jnp.take_along_axis(scores, top_idx, axis=-1)
        gates = jnp.sum(jax.nn.one_hot(top_idx, E, dtype=scores.dtype) * top_scores[..., None], axis=-2)
        xf = x.reshape(-1, D)
        gf = gates.reshape(-1, E).T

        def body(acc, ws):
            w1, w2, w3, g = ws
            return (acc + _swiglu(xf, w1, w2, w3) * g[:, None], None)
        routed_out, _ = jax.lax.scan(body, jnp.zeros_like(xf), (routed_w1, routed_w2, routed_w3, gf))
        return shared_out + routed_out.reshape(x.shape)
    x = x + jnp.tanh(g_xattn[0]) * _L0_xattn_ref(ctx_1024, ctx_1024, _layernorm(x, axis=-1), L0_xattn_Wk, L0_xattn_Wv, L0_xattn_bv, L0_xattn_Wq, L0_xattn_bq, L0_xattn_Wo, L0_xattn_bo)
    x = x + jnp.tanh(g_ffn[0]) * _L0_ffn_ref(_layernorm(x, axis=-1), L0_ffn_router_w, L0_ffn_expert_bias, L0_ffn_shared_w1, L0_ffn_shared_w2, L0_ffn_shared_w3, L0_ffn_routed_w1, L0_ffn_routed_w2, L0_ffn_routed_w3)
    return x

_drawn_inputs = setup_inputs


def setup_inputs(seed=0):
    import zlib

    import numpy as np

    out = dict(_drawn_inputs(seed))
    spreads = {'L0_xattn_bv': (0.0, 0.1),
     'L0_xattn_bq': (0.0, 0.385),
     'L0_xattn_bo': (0.0, 0.1),
     'L0_ffn_expert_bias': (0.0, 0.8)}
    factors = {'L0_ffn_router_w': 8.0,
     'L0_ffn_shared_w1': 5.588,
     'L0_ffn_shared_w2': 5.603,
     'L0_ffn_shared_w3': 5.583,
     'L0_ffn_routed_w1': 8.0,
     'L0_ffn_routed_w2': 8.0,
     'L0_ffn_routed_w3': 8.0}
    for name, (base, spread) in spreads.items():
        noise = np.random.default_rng([zlib.crc32(name.encode()), seed]).standard_normal(out[name].shape)
        drawn = base * np.exp(spread * noise) if base else spread * noise
        out[name] = jnp.asarray(drawn.astype(out[name].dtype))
    for name, factor in factors.items():
        out[name] = (out[name] * factor).astype(out[name].dtype)
    return out
```

```python
from contextlib import ExitStack

import concourse.bass as bass
from concourse import mybir

F32 = mybir.dt.float32
ALU = mybir.AluOpType
ACT = mybir.ActivationFunctionType
AX = mybir.AxisListType.X

P = 128


def flamingo_block(
    nc: bass.Bass,
    x: bass.AP,
    ctx_in: bass.AP,
    g_xattn: bass.AP,
    g_ffn: bass.AP,
    Wk: bass.AP,
    Wv: bass.AP,
    bv: bass.AP,
    Wq: bass.AP,
    bq: bass.AP,
    Wo: bass.AP,
    bo: bass.AP,
    router_w: bass.AP,
    expert_bias: bass.AP,
    shared_w1: bass.AP,
    shared_w2: bass.AP,
    shared_w3: bass.AP,
    routed_w1: bass.AP,
    routed_w2: bass.AP,
    routed_w3: bass.AP,
    out: bass.AP,
):
    B, S, D = x.shape
    E = router_w.shape[1]
    H = shared_w1.shape[2]
    HJ = H // P
    HALF = B // 2
    SCALE = float(D) ** -0.5
    EPS = 1e-5
    BIG = 3.0e38
    assert S == P and D == P and HALF * P == 512

    with ExitStack() as stack:
        def sb(name, shape, dt=F32):
            return stack.enter_context(nc.sbuf_tensor(name, shape, dt))

        def sem(name):
            return stack.enter_context(nc.semaphore(name))

        bank = [stack.enter_context(nc.psum_tensor(f"bank{i}", [P, 512], F32)) for i in range(8)]

        x_sb = sb("x_sb", [P, B, D])
        ctx_sb = sb("ctx_sb", [P, B, D])
        wq_sb = sb("wq_sb", [P, D])
        wk_sb = sb("wk_sb", [P, D])
        wv_sb = sb("wv_sb", [P, D])
        wo_sb = sb("wo_sb", [P, D])
        bq_col = sb("bq_col", [P, 1])
        bv_col = sb("bv_col", [P, 1])
        bo_row = sb("bo_row", [1, D])
        gains = sb("gains", [P, 2])
        rw_sb = sb("rw_sb", [P, E])
        ebias = sb("ebias", [P, E])
        w1s = sb("w1s", [P, H])
        w2s = sb("w2s", [P, H])
        w3s = sb("w3s", [P, HJ, D])
        wring = sb("wring", [P, 2, 3, P])
        ident = sb("ident", [P, P])
        ones_row = sb("ones_row", [1, P])
        ones_mat = sb("ones_mat", [P, P])
        bv_mat = sb("bv_mat", [P, P])
        neg_half = sb("neg_half", [P, HALF])
        rev_index = sb("rev_index", [P, E])
        woT = sb("woT", [P, D])
        qk_w = sb("qk_w", [P, D])
        vo_w = sb("vo_w", [P, D])
        u_col = sb("u_col", [P, 1])
        tanh_g = sb("tanh_g", [P, 2])
        out_bias = sb("out_bias", [P, D])
        stats = sb("stats", [P, 2, B, 6])
        mean_var = sb("mean_var", [P, 2, B, 2])
        var_eps = sb("var_eps", [P, 2, B])
        rstd = sb("rstd", [P, 2, B])
        xn = sb("xn", [P, B, D])
        xb = sb("xb", [P, B, D])
        ctxT = sb("ctxT", [P, B, S])
        xnT = sb("xnT", [P, B, S])
        gT = sb("gT", [P, B, S])
        vo = sb("vo", [P, B, D])
        row_max = sb("row_max", [P, B])
        neg_max = sb("neg_max", [P, B])
        probs = sb("probs", [P, B, S])
        row_sum = sb("row_sum", [P, B])
        inv_sum = sb("inv_sum", [P, B])
        coef = sb("coef", [P, B])
        probsT = sb("probsT", [P, B, S])
        x2 = sb("x2", [P, B, D])
        x2n = sb("x2n", [P, B, D])
        x2nT = sb("x2nT", [P, B, S])
        scores = sb("scores", [P, B, E])
        sel = sb("sel", [P, 2, B, E])
        best = sb("best", [P, 2, B])
        is_best = sb("is_best", [P, 2, B, E])
        rank_of = sb("rank_of", [P, 2, B, E])
        first = sb("first", [P, 2, B])
        onehot = sb("onehot", [P, 2, B, E])
        chosen = sb("chosen", [P, B, E])
        gates = sb("gates", [P, E, B])
        silu_t = sb("silu_t", [P, 2, 512])
        hid = sb("hid", [P, HJ, 512])
        acc = sb("acc", [P, B, D])

        w_loaded = sem("w_loaded")
        ctx_loaded = [sem(f"ctx_loaded{i}") for i in range(2)]
        x_loaded = [sem(f"x_loaded{i}") for i in range(2)]
        small_loaded = sem("small_loaded")
        gains_loaded = sem("gains_loaded")
        router_loaded = sem("router_loaded")
        shared_loaded = sem("shared_loaded")
        expert_loaded = [sem(f"expert_loaded{i}") for i in range(2)]
        zeroed = sem("zeroed")
        consts_ready = sem("consts_ready")
        bv_ready = sem("bv_ready")
        tanh_ready = sem("tanh_ready")
        wo_turned = sem("wo_turned")
        woT_ready = sem("woT_ready")
        fused_done = sem("fused_done")
        fused_ready = sem("fused_ready")
        bias_ready = sem("bias_ready")
        ctx_turned = sem("ctx_turned")
        ctxT_ready = sem("ctxT_ready")
        stats_ready = sem("stats_ready")
        moments_ready = sem("moments_ready")
        var_ready = sem("var_ready")
        rstd_ready = sem("rstd_ready")
        xn_ready = sem("xn_ready")
        xn_turned = sem("xn_turned")
        xnT_ready = sem("xnT_ready")
        xb_ready = sem("xb_ready")
        vo_done = sem("vo_done")
        vo_ready = sem("vo_ready")
        g_done = sem("g_done")
        g_ready = sem("g_ready")
        scores_done = sem("scores_done")
        max_ready = sem("max_ready")
        neg_ready = sem("neg_ready")
        probs_ready = sem("probs_ready")
        inv_ready = sem("inv_ready")
        coef_ready = sem("coef_ready")
        probs_turned = sem("probs_turned")
        probsT_ready = sem("probsT_ready")
        pv_done = sem("pv_done")
        x2_ready = sem("x2_ready")
        x2n_ready = sem("x2n_ready")
        x2n_turned = sem("x2n_turned")
        x2nT_ready = sem("x2nT_ready")
        logits_done = sem("logits_done")
        sigmoid_ready = sem("sigmoid_ready")
        route_step = sem("route_step")
        gates_ready = sem("gates_ready")
        up_done = sem("up_done")
        silu_ready = sem("silu_ready")
        hid_ready = sem("hid_ready")
        down_done = sem("down_done")
        acc_ready = sem("acc_ready")
        r_up_done = sem("r_up_done")
        r_silu_ready = sem("r_silu_ready")
        r_hid_ready = sem("r_hid_ready")
        r_down_done = sem("r_down_done")
        r_acc_ready = sem("r_acc_ready")
        stored = sem("stored")

        block = stack.enter_context(nc.Block())
        x_dram = x.rearrange("b s d -> s b d")
        c_dram = ctx_in.rearrange("b s d -> s b d")
        o_dram = out.rearrange("b s d -> s b d")

        def halves(h):
            return slice(h * HALF, (h + 1) * HALF)

        @block.sync
        def _(sp):
            for h in range(2):
                sp.dma_start(ctx_sb[:, halves(h), :], c_dram[:, halves(h), :]).then_inc(ctx_loaded[h], 16)
                sp.dma_start(x_sb[:, halves(h), :], x_dram[:, halves(h), :]).then_inc(x_loaded[h], 16)
            sp.dma_start(w1s[:, :], shared_w1[0]).then_inc(shared_loaded, 16)
            sp.dma_start(w2s[:, :], shared_w2[0]).then_inc(shared_loaded, 16)
            sp.dma_start(w3s[:, :, :], shared_w3[0].rearrange("(j h) d -> h j d", h=P)).then_inc(shared_loaded, 16)
            with sp.Fori(0, E // 2) as i:
                for s in range(2):
                    sp.wait_ge(r_acc_ready, i * 16 + 8 * s)
                    for m, w in enumerate((routed_w1, routed_w2, routed_w3)):
                        sp.dma_start(wring[:, s, m, :], w[bass.ds(i * 2 + s, 1), :, :].rearrange("e a b -> (e a) b"))\
                          .then_inc(expert_loaded[s], 16)
            for h in range(2):
                sp.wait_ge(r_acc_ready, 8 * E)
                sp.dma_start(o_dram[:, halves(h), :], acc[:, halves(h), :]).then_inc(stored, 16)
            sp.wait_ge(stored, 32)

        @block.gpsimd
        def _(pool):
            pool.dma_start(gains[:, 0:1], g_xattn.rearrange("(a n) -> a n", a=1).to_broadcast([P, 1])).then_inc(gains_loaded, 16)
            pool.dma_start(gains[:, 1:2], g_ffn.rearrange("(a n) -> a n", a=1).to_broadcast([P, 1])).then_inc(gains_loaded, 16)
            pool.dma_start(rw_sb[:, :], router_w).then_inc(router_loaded, 16)
            pool.dma_start(ebias[:, :], expert_bias.rearrange("(a n) -> a n", a=1).to_broadcast([P, E])).then_inc(router_loaded, 16)
            pool.memset(ident[:, :], 0.0).then_inc(zeroed, 1)
            pool.memset(ones_row[:, :], 1.0).then_inc(consts_ready, 1)
            pool.memset(ones_mat[:, :], 1.0).then_inc(consts_ready, 1)
            pool.memset(neg_half[:, :], -0.5).then_inc(consts_ready, 1)
            pool.iota(rev_index[:, :], pattern=[[-1, E]], base=E, channel_multiplier=0,
                      allow_small_or_imprecise_dtypes=True).then_inc(consts_ready, 1)
            pool.wait_ge(zeroed, 1)
            pool.affine_select(out=ident[:, :], in_=ident[:, :], compare_op=ALU.not_equal, fill=1.0,
                               base=0, pattern=[[-1, P]], channel_multiplier=1).then_inc(consts_ready, 1)
            for n in range(2):
                for h in range(2):
                    k = 2 * n + h
                    pool.wait_ge(moments_ready, HALF * (k + 1))
                    pool.tensor_scalar(var_eps[:, n, halves(h)], mean_var[:, n, halves(h), 1], EPS, None, ALU.add)\
                        .then_inc(var_ready, 1)
                    pool.wait_ge(var_ready, k + 1)
                    pool.wait_ge(consts_ready, 5)
                    pool.tensor_tensor(rstd[:, n, halves(h)], var_eps[:, n, halves(h)], neg_half[:, :], ALU.pow)\
                        .then_inc(rstd_ready, 1)
                if n == 0:
                    pool.wait_ge(bias_ready, 1)
                    for h in range(2):
                        pool.wait_ge(x_loaded[h], 16)
                        pool.tensor_tensor(xb[:, halves(h), :], x_sb[:, halves(h), :],
                                           out_bias[:, None, :].to_broadcast([P, HALF, D]), ALU.add)\
                            .then_inc(xb_ready, 1)

        @block.scalar
        def _(act):
            act.dma_start(wo_sb[:, :], Wo).then_inc(w_loaded, 16)
            act.dma_start(wq_sb[:, :], Wq).then_inc(w_loaded, 16)
            act.dma_start(wk_sb[:, :], Wk).then_inc(w_loaded, 16)
            act.dma_start(wv_sb[:, :], Wv).then_inc(w_loaded, 16)
            act.dma_start(bq_col[:, :], bq.rearrange("(p a) -> p a", a=1)).then_inc(small_loaded, 16)
            act.dma_start(bv_col[:, :], bv.rearrange("(p a) -> p a", a=1)).then_inc(small_loaded, 16)
            act.dma_start(bo_row[:, :], bo.rearrange("(a n) -> a n", a=1)).then_inc(small_loaded, 16)
            act.wait_ge(gains_loaded, 32)
            nc.scalar.activation(tanh_g[:, :], gains[:, :], ACT.Tanh).then_inc(tanh_ready, 1)
            act.wait_ge(wo_turned, 1)
            nc.scalar.copy(woT[:, :], bank[0][:, 0:128]).then_inc(woT_ready, 1)
            act.wait_ge(fused_done, 1)
            nc.scalar.copy(qk_w[:, :], bank[1][:, 0:128]).then_inc(fused_ready, 1)
            nc.scalar.copy(u_col[:, :], bank[1][:, 128:129]).then_inc(fused_ready, 1)
            act.wait_ge(fused_done, 2)
            nc.scalar.copy(vo_w[:, :], bank[0][:, 128:256]).then_inc(fused_ready, 1)
            act.wait_ge(tanh_ready, 1)
            nc.scalar.mul(out_bias[:, :], bank[0][:, 256:384], tanh_g[:, 0:1]).then_inc(bias_ready, 1)
            for h in range(2):
                act.wait_ge(ctx_turned, h + 1)
                nc.scalar.copy(ctxT[:, halves(h), :], bank[2 + h][:, :].rearrange("p (b s) -> p b s", b=HALF)).then_inc(ctxT_ready, 1)
            for h in range(2):
                act.wait_ge(xn_turned, h + 1)
                nc.scalar.copy(xnT[:, halves(h), :], bank[4 + h][:, :].rearrange("p (b s) -> p b s", b=HALF)).then_inc(xnT_ready, 1)
            for h in range(2):
                act.wait_ge(vo_done, h + 1)
                nc.scalar.copy(vo[:, halves(h), :], bank[6 + h][:, :].rearrange("p (b s) -> p b s", b=HALF)).then_inc(vo_ready, 1)
            for h in range(2):
                act.wait_ge(neg_ready, h + 1)
                for b in range(HALF):
                    k = HALF * h + b
                    nc.scalar.activation(probs[:, k, :], bank[2 + h][:, b * S:(b + 1) * S], ACT.Exp,
                                         bias=neg_max[:, k:k + 1], scale=SCALE,
                                         accum_out=row_sum[:, k:k + 1]).then_inc(probs_ready, 1)
            for h in range(2):
                act.wait_ge(x2n_turned, h + 1)
                nc.scalar.copy(x2nT[:, halves(h), :], bank[h][:, :].rearrange("p (b s) -> p b s", b=HALF)).then_inc(x2nT_ready, 1)
            act.wait_ge(logits_done, 1)
            nc.scalar.activation(scores[:, :, :], bank[2][:, 0:B * E].rearrange("p (b e) -> p b e", b=B), ACT.Sigmoid)\
                .then_inc(sigmoid_ready, 1)
            for k in range(2 * HJ):
                act.wait_ge(up_done, k + 1)
                if k >= 2:
                    act.wait_ge(hid_ready, k - 1)
                nc.scalar.activation(silu_t[:, k % 2, :], bank[4 + 2 * (k % 2)][:, :], ACT.Silu).then_inc(silu_ready, 1)
            with act.Fori(0, E // 2) as i:
                for s in range(2):
                    for t in range(2):
                        n = 2 * s + t
                        act.wait_ge(r_up_done, i * 4 + (n + 1))
                        act.wait_ge(hid_ready, 2 * HJ)
                        act.wait_ge(r_hid_ready, i * 4 + max(n - 1, 0))
                        nc.scalar.activation(silu_t[:, t, :], bank[4 + 2 * t][:, :], ACT.Silu).then_inc(r_silu_ready, 1)

        @block.vector
        def _(dve):
            def moments(n, src, h):
                for b in range(HALF):
                    k = HALF * h + b
                    nc.vector.bn_stats(stats[:, n, k, :], src[:, k, :]).then_inc(stats_ready, 1)
                for b in range(HALF):
                    k = HALF * h + b
                    dve.wait_ge(stats_ready, B * n + k + 1)
                    nc.vector.bn_aggr(mean_var[:, n, k, :], stats[:, n, k, :]).then_inc(moments_ready, 1)

            def normalise(n, src, dst, h, ready):
                dve.wait_ge(rstd_ready, 2 * n + h + 1)
                for b in range(HALF):
                    k = HALF * h + b
                    nc.vector.tensor_scalar(dst[:, k, :], src[:, k, :], mean_var[:, n, k, 0:1], rstd[:, n, k:k + 1],
                                            ALU.subtract, ALU.mult).then_inc(ready, 1)

            for h in range(2):
                dve.wait_ge(x_loaded[h], 16)
                moments(0, x_sb, h)
            dve.wait_ge(small_loaded, 48)
            dve.wait_ge(consts_ready, 5)
            nc.vector.tensor_scalar(bv_mat[:, :], ones_mat[:, :], bv_col[:, 0:1], None, ALU.mult).then_inc(bv_ready, 1)
            for h in range(2):
                dve.wait_ge(moments_ready, B)
                normalise(0, x_sb, xn, h, xn_ready)
            for h in range(2):
                dve.wait_ge(g_done, h + 1)
                dve.wait_ge(fused_ready, 3)
                nc.vector.tensor_scalar(gT[:, halves(h), :], bank[h][:, :].rearrange("p (b s) -> p b s", b=HALF),
                                        u_col[:, 0:1], None, ALU.add).then_inc(g_ready, 1)
            for h in range(2):
                dve.wait_ge(scores_done, h + 1)
                nc.vector.reduce_max(row_max[:, halves(h)], bank[2 + h][:, :].rearrange("p (b s) -> p b s", b=HALF), AX)\
                    .then_inc(max_ready, 1)
                dve.wait_ge(max_ready, h + 1)
                nc.vector.tensor_scalar(neg_max[:, halves(h)], row_max[:, halves(h)], -SCALE, None, ALU.mult).then_inc(neg_ready, 1)
            for h in range(2):
                dve.wait_ge(probs_ready, HALF * (h + 1))
                nc.vector.reciprocal(inv_sum[:, halves(h)], row_sum[:, halves(h)]).then_inc(inv_ready, 1)
                dve.wait_ge(tanh_ready, 1)
                dve.wait_ge(inv_ready, h + 1)
                nc.vector.tensor_scalar(coef[:, halves(h)], inv_sum[:, halves(h)], tanh_g[:, 0:1], None, ALU.mult).then_inc(coef_ready, 1)
                dve.wait_ge(probs_turned, h + 1)
                nc.vector.tensor_copy(probsT[:, halves(h), :], bank[4 + h][:, :].rearrange("p (b s) -> p b s", b=HALF)).then_inc(probsT_ready, 1)
            for h in range(2):
                dve.wait_ge(pv_done, h + 1)
                dve.wait_ge(coef_ready, h + 1)
                dve.wait_ge(xb_ready, h + 1)
                for b in range(HALF):
                    k = HALF * h + b
                    nc.vector.scalar_tensor_tensor(x2[:, k, :], bank[6 + h][:, b * D:(b + 1) * D], coef[:, k:k + 1],
                                                   xb[:, k, :], ALU.mult, ALU.add).then_inc(x2_ready, 1)
                dve.wait_ge(x2_ready, HALF * (h + 1))
                moments(1, x2, h)
            dve.wait_ge(moments_ready, 2 * B)
            for h in range(2):
                normalise(1, x2, x2n, h, x2n_ready)

            steps = [0]

            def step(ins):
                ins.then_inc(route_step, 1)
                steps[0] += 1
                dve.wait_ge(route_step, steps[0])

            def per_expert(a):
                return a[:, :, None].to_broadcast([P, B, E])

            idx = rev_index[:, None, :].to_broadcast([P, B, E])
            dve.wait_ge(sigmoid_ready, 1)
            dve.wait_ge(router_loaded, 32)
            step(nc.vector.tensor_tensor(sel[:, 0], scores[:, :, :], ebias[:, None, :].to_broadcast([P, B, E]), ALU.add))
            for k in range(2):
                step(nc.vector.reduce_max(best[:, k], sel[:, k], AX))
                step(nc.vector.tensor_tensor(is_best[:, k], sel[:, k], per_expert(best[:, k]), ALU.is_equal))
                step(nc.vector.tensor_tensor(rank_of[:, k], is_best[:, k], idx, ALU.mult))
                step(nc.vector.reduce_max(first[:, k], rank_of[:, k], AX))
                step(nc.vector.tensor_tensor(onehot[:, k], idx, per_expert(first[:, k]), ALU.is_equal))
                if k == 0:
                    step(nc.vector.scalar_tensor_tensor(sel[:, 1], onehot[:, 0], -BIG, sel[:, 0], ALU.mult, ALU.add))
            step(nc.vector.tensor_tensor(chosen[:, :, :], onehot[:, 0], onehot[:, 1], ALU.add))
            step(nc.vector.tensor_tensor(chosen[:, :, :], chosen[:, :, :], scores[:, :, :], ALU.mult))
            nc.vector.tensor_scalar(gates[:, :, :], chosen[:, :, :].rearrange("p b e -> p e b"), tanh_g[:, 1:2], None, ALU.mult)\
                .then_inc(gates_ready, 1)

            for t in range(2):
                for j in range(HJ):
                    k = HJ * t + j
                    dve.wait_ge(silu_ready, k + 1)
                    if t == 1:
                        dve.wait_ge(down_done, 1)
                    nc.vector.tensor_tensor(hid[:, j, :], silu_t[:, k % 2, :], bank[5 + 2 * (k % 2)][:, :], ALU.mult)\
                        .then_inc(hid_ready, 1)
                dve.wait_ge(down_done, t + 1)
                nc.vector.scalar_tensor_tensor(acc[:, halves(t), :], bank[t][:, :].rearrange("p (b s) -> p b s", b=HALF), tanh_g[:, 1:2],
                                               x2[:, halves(t), :], ALU.mult, ALU.add).then_inc(acc_ready, 1)
            dve.wait_ge(acc_ready, 2)
            dve.wait_ge(gates_ready, 1)
            with dve.Fori(0, E // 2) as i:
                for s in range(2):
                    for t in range(2):
                        n = 2 * s + t
                        dve.wait_ge(r_silu_ready, i * 4 + (n + 1))
                        dve.wait_ge(r_down_done, i * 4 + max(n - 1, 0))
                        nc.vector.tensor_tensor(hid[:, t, :], silu_t[:, t, :], bank[5 + 2 * t][:, :], ALU.mult)\
                            .then_inc(r_hid_ready, 1)
                        dve.wait_ge(r_down_done, i * 4 + (n + 1))
                        dve.wait_ge(r_acc_ready, i * 16 + 4 * n)
                        for b in range(HALF):
                            k = HALF * t + b
                            nc.vector.scalar_tensor_tensor(
                                acc[:, k, :], bank[t][:, b * D:(b + 1) * D],
                                gates[:, bass.ds(i * 2 + s, 1), k], acc[:, k, :],
                                ALU.mult, ALU.add).then_inc(r_acc_ready, 1)

        @block.tensor
        def _(pe):
            pe.wait_ge(consts_ready, 5)
            pe.wait_ge(w_loaded, 64)
            pe.wait_ge(small_loaded, 48)
            nc.tensor.transpose(bank[0][:, 0:128], wo_sb[:, :], ident[:, :]).then_inc(wo_turned, 1)
            nc.tensor.matmul(bank[1][:, 0:128], wq_sb[:, :], wk_sb[:, :], start=True, stop=True)
            nc.tensor.matmul(bank[1][:, 128:129], wk_sb[:, :], bq_col[:, :], start=True, stop=True).then_inc(fused_done, 1)
            pe.wait_ge(woT_ready, 1)
            nc.tensor.matmul(bank[0][:, 128:256], wv_sb[:, :], woT[:, :], start=True, stop=True)
            pe.wait_ge(bv_ready, 1)
            nc.tensor.matmul(bank[0][:, 256:384], bv_mat[:, :], woT[:, :], start=True, stop=False)
            nc.tensor.matmul(bank[0][:, 256:384], ones_row[:, :], bo_row[:, :], start=False, stop=True).then_inc(fused_done, 1)

            def turn(dst, src, h, done):
                for b in range(HALF):
                    last = nc.tensor.transpose(dst[:, b * P:(b + 1) * P], src[:, HALF * h + b, :], ident[:, :])
                last.then_inc(done, 1)

            for h in range(2):
                pe.wait_ge(ctx_loaded[h], 16)
                turn(bank[2 + h], ctx_sb, h, ctx_turned)
            for h in range(2):
                pe.wait_ge(xn_ready, HALF * (h + 1))
                turn(bank[4 + h], xn, h, xn_turned)
            pe.wait_ge(fused_ready, 3)
            pe.wait_ge(bias_ready, 1)
            for h in range(2):
                pe.wait_ge(ctxT_ready, h + 1)
                for b in range(HALF):
                    last = nc.tensor.matmul(bank[6 + h][:, b * P:(b + 1) * P], ctxT[:, HALF * h + b, :], vo_w[:, :], start=True, stop=True)
                last.then_inc(vo_done, 1)
            for h in range(2):
                pe.wait_ge(xnT_ready, h + 1)
                nc.tensor.matmul(bank[h][:, :], qk_w[:, :], xnT[:, halves(h), :], start=True, stop=True).then_inc(g_done, 1)
            for h in range(2):
                pe.wait_ge(g_ready, h + 1)
                for b in range(HALF):
                    k = HALF * h + b
                    last = nc.tensor.matmul(bank[2 + h][:, b * P:(b + 1) * P], gT[:, k, :], ctxT[:, k, :], start=True, stop=True)
                last.then_inc(scores_done, 1)
            for h in range(2):
                pe.wait_ge(probs_ready, HALF * (h + 1))
                turn(bank[4 + h], probs, h, probs_turned)
            for h in range(2):
                pe.wait_ge(probsT_ready, h + 1)
                pe.wait_ge(vo_ready, h + 1)
                for b in range(HALF):
                    k = HALF * h + b
                    last = nc.tensor.matmul(bank[6 + h][:, b * P:(b + 1) * P], probsT[:, k, :], vo[:, k, :], start=True, stop=True)
                last.then_inc(pv_done, 1)
            for h in range(2):
                pe.wait_ge(x2n_ready, HALF * (h + 1))
                turn(bank[h], x2n, h, x2n_turned)
            pe.wait_ge(x2nT_ready, 2)
            pe.wait_ge(router_loaded, 32)
            for k in range(B):
                last = nc.tensor.matmul(bank[2][:, k * E:(k + 1) * E], x2nT[:, k, :], rw_sb[:, :], start=True, stop=True)
            last.then_inc(logits_done, 1)

            pe.wait_ge(shared_loaded, 48)
            for t in range(2):
                for j in range(HJ):
                    k = HJ * t + j
                    if k >= 2:
                        pe.wait_ge(hid_ready, k - 1)
                    a = bank[4 + 2 * (k % 2)]
                    u = bank[5 + 2 * (k % 2)]
                    xt = x2nT[:, halves(t), :]
                    nc.tensor.matmul(a[:, :], w1s[:, j * P:(j + 1) * P], xt, start=True, stop=True)
                    nc.tensor.matmul(u[:, :], w2s[:, j * P:(j + 1) * P], xt, start=True, stop=True).then_inc(up_done, 1)
                pe.wait_ge(hid_ready, HJ * (t + 1))
                for b in range(HALF):
                    for j in range(HJ):
                        last = nc.tensor.matmul(bank[t][:, b * P:(b + 1) * P], hid[:, j, b * P:(b + 1) * P], w3s[:, j, :],
                                                start=(j == 0), stop=(j == HJ - 1))
                last.then_inc(down_done, 1)
            pe.wait_ge(acc_ready, 2)
            with pe.Fori(0, E // 2) as i:
                for s in range(2):
                    pe.wait_ge(expert_loaded[s], i * 48 + 48)
                    for t in range(2):
                        n = 2 * s + t
                        pe.wait_ge(r_hid_ready, i * 4 + max(n - 1, 0))
                        xt = x2nT[:, halves(t), :]
                        nc.tensor.matmul(bank[4 + 2 * t][:, :], wring[:, s, 0, :], xt, start=True, stop=True)
                        nc.tensor.matmul(bank[5 + 2 * t][:, :], wring[:, s, 1, :], xt, start=True, stop=True).then_inc(r_up_done, 1)
                    for t in range(2):
                        n = 2 * s + t
                        pe.wait_ge(r_hid_ready, i * 4 + (n + 1))
                        pe.wait_ge(r_acc_ready, i * 16 + max(4 * (n - 1), 0))
                        for b in range(HALF):
                            last = nc.tensor.matmul(bank[t][:, b * P:(b + 1) * P], hid[:, t, b * P:(b + 1) * P],
                                                    wring[:, s, 2, :], start=True, stop=True)
                        last.then_inc(r_down_done, 1)


_INS = ['x', 'ctx_1024', 'g_xattn', 'g_ffn', 'L0_xattn_Wk', 'L0_xattn_Wv', 'L0_xattn_bv', 'L0_xattn_Wq',
        'L0_xattn_bq', 'L0_xattn_Wo', 'L0_xattn_bo', 'L0_ffn_router_w', 'L0_ffn_expert_bias', 'L0_ffn_shared_w1',
        'L0_ffn_shared_w2', 'L0_ffn_shared_w3', 'L0_ffn_routed_w1', 'L0_ffn_routed_w2', 'L0_ffn_routed_w3']


def kernel(**inputs):
    import numpy as _np
    import concourse.bacc as _bacc
    from concourse import mybir as _mybir
    from concourse.bass_utils import run_bass_kernel_spmd as _run

    nc = _bacc.Bacc("TRN2", target_bir_lowering=False, num_devices=1)
    arrays, args = {}, []
    for name in _INS:
        a = _np.ascontiguousarray(inputs[name])
        arrays[f"in_{name}_dram"] = a
        args.append(nc.dram_tensor(f"in_{name}_dram", a.shape, _mybir.dt.from_np(a.dtype), kind="ExternalInput").ap())
    shape = inputs["x"].shape
    args.append(nc.dram_tensor("out_0_dram", shape, _mybir.dt.float32, kind="ExternalOutput").ap())
    flamingo_block(nc, *args)
    r = _run(nc, [arrays], core_ids=[0])
    return r.results[0]["out_0_dram"]
```

```python
from contextlib import ExitStack

import concourse.bass as bass
from concourse import mybir

F32 = mybir.dt.float32
BF16 = mybir.dt.bfloat16
I32 = mybir.dt.int32
U32 = mybir.dt.uint32
ALU = mybir.AluOpType
ACT = mybir.ActivationFunctionType
AX = mybir.AxisListType.X

P = 128


def flamingo_block(
    nc: bass.Bass,
    x: bass.AP,
    ctx_in: bass.AP,
    g_xattn: bass.AP,
    g_ffn: bass.AP,
    Wk: bass.AP,
    Wv: bass.AP,
    bv: bass.AP,
    Wq: bass.AP,
    bq: bass.AP,
    Wo: bass.AP,
    bo: bass.AP,
    router_w: bass.AP,
    expert_bias: bass.AP,
    shared_w1: bass.AP,
    shared_w2: bass.AP,
    shared_w3: bass.AP,
    routed_w: bass.AP,
    out: bass.AP,
):
    B, S, D = x.shape
    E = router_w.shape[1]
    H = shared_w1.shape[2]
    HJ = H // P
    HALF = B // 2
    SCALE = float(D) ** -0.5
    EPS = 1e-5
    BIG = 3.0e38
    TOP = 2
    TILES = TOP * B * S // P + E - 1
    CONSTS = 9
    GROUP = 4
    GROUPS = -(-TILES // GROUP)
    UP_RING = 4
    assert S == P and D == P and HALF * P == 512

    with ExitStack() as stack:
        def sb(name, shape, dt=F32):
            return stack.enter_context(nc.sbuf_tensor(name, shape, dt))

        def sem(name):
            return stack.enter_context(nc.semaphore(name))

        bank = [stack.enter_context(nc.psum_tensor(f"bank{i}", [P, 512], F32)) for i in range(8)]

        x_sb = sb("x_sb", [P, B, D])
        ctx_sb = sb("ctx_sb", [P, B, D])
        wq_sb = sb("wq_sb", [P, D])
        wk_sb = sb("wk_sb", [P, D])
        wv_sb = sb("wv_sb", [P, D])
        wo_sb = sb("wo_sb", [P, D])
        bq_col = sb("bq_col", [P, 1])
        bv_col = sb("bv_col", [P, 1])
        bo_row = sb("bo_row", [1, D])
        gains = sb("gains", [P, 2])
        rw_sb = sb("rw_sb", [P, E])
        ebias = sb("ebias", [P, E])
        w1s = sb("w1s", [P, H])
        w2s = sb("w2s", [P, H])
        w3s = sb("w3s", [P, HJ, D])
        ident = sb("ident", [P, P])
        ones_row = sb("ones_row", [1, P])
        ones_mat = sb("ones_mat", [P, P])
        bv_mat = sb("bv_mat", [P, P])
        neg_half = sb("neg_half", [P, HALF])
        rev_index = sb("rev_index", [P, E])
        zeros = sb("zeros", [P, D])
        ones_bf = sb("ones_bf", [P, P], BF16)
        earlier_token = sb("earlier_token", [P, P], BF16)
        expert_order = sb("expert_order", [E, 2, E])
        tile_start = sb("tile_start", [1, TILES])
        woT = sb("woT", [P, D])
        qk_w = sb("qk_w", [P, D])
        vo_w = sb("vo_w", [P, D])
        u_col = sb("u_col", [P, 1])
        tanh_g = sb("tanh_g", [P, 2])
        out_bias = sb("out_bias", [P, D])
        stats = sb("stats", [P, 2, B, 6])
        mean_var = sb("mean_var", [P, 2, B, 2])
        var_eps = sb("var_eps", [P, 2, B])
        rstd = sb("rstd", [P, 2, B])
        xn = sb("xn", [P, B, D])
        xb = sb("xb", [P, B, D])
        ctxT = sb("ctxT", [P, B, S])
        xnT = sb("xnT", [P, B, S])
        gT = sb("gT", [P, B, S])
        vo = sb("vo", [P, B, D])
        row_max = sb("row_max", [P, B])
        neg_max = sb("neg_max", [P, B])
        probs = sb("probs", [P, B, S])
        row_sum = sb("row_sum", [P, B])
        inv_sum = sb("inv_sum", [P, B])
        coef = sb("coef", [P, B])
        probsT = sb("probsT", [P, B, S])
        x2 = sb("x2", [P, B, D])
        x2n = sb("x2n", [P, B, D])
        x2nT = sb("x2nT", [P, B, S])
        scores = sb("scores", [P, B, E])
        sel = sb("sel", [P, 2, B, E])
        best = sb("best", [P, 2, B])
        is_best = sb("is_best", [P, 2, B, E])
        rank_of = sb("rank_of", [P, 2, B, E])
        first = sb("first", [P, 2, B])
        onehot = sb("onehot", [P, 2, B, E])
        chosen = sb("chosen", [P, B, E], BF16)
        raised_count = sb("raised_count", [E, P], I32)
        tile_count = sb("tile_count", [E, P], I32)
        padded_count = sb("padded_count", [E, P])
        picked_rank = sb("picked_rank", [P, TOP * B, E])
        slot_f = sb("slot_f", [P, TOP * B])
        slot = sb("slot", [P, TOP * B], U32)
        passed = sb("passed", [1, TILES, E])
        tile_expert_f = sb("tile_expert_f", [1, TILES])
        tile_expert = sb("tile_expert", [1, TILES], I32)
        picked_score = sb("picked_score", [P, TOP, B, E])
        gate_raw = sb("gate_raw", [P, TOP * B])
        gates = sb("gates", [P, TOP * B])
        silu_t = sb("silu_t", [P, 2, 512])
        hid = sb("hid", [P, HJ, 512])
        acc = sb("acc", [P, B, D])
        tile_w = sb("tile_w", [P, TILES, 3 * P])
        tile_x = sb("tile_x", [P, TILES, D])
        tile_xT = sb("tile_xT", [P, GROUPS, GROUP * P])
        tile_silu = sb("tile_silu", [P, 2, P])
        tile_hid = sb("tile_hid", [P, 3, P])
        tile_y = sb("tile_y", [P, TILES, D])
        picked_y = sb("picked_y", [P, TOP * B, D])
        part = sb("part", [P, B, D])
        final = sb("final", [P, B, D])
        sorted_x = nc.dram_tensor("sorted_x", [TILES * P, D], F32).ap()
        sorted_y = nc.dram_tensor("sorted_y", [TILES * P, D], F32).ap()

        w_loaded = sem("w_loaded")
        ctx_loaded = [sem(f"ctx_loaded{i}") for i in range(2)]
        x_loaded = [sem(f"x_loaded{i}") for i in range(2)]
        small_loaded = sem("small_loaded")
        gains_loaded = sem("gains_loaded")
        router_loaded = sem("router_loaded")
        shared_loaded = sem("shared_loaded")
        rows_zeroed = sem("rows_zeroed")
        rows_scattered = sem("rows_scattered")
        tile_x_loaded = [sem(f"tile_x_loaded{g}") for g in range(GROUPS)]
        tile_w_loaded = [sem(f"tile_w_loaded{j}") for j in range(TILES)]
        y_stored = sem("y_stored")
        y_gathered = [sem(f"y_gathered{b}") for b in range(B)]
        chosen_ready = sem("chosen_ready")
        counts_done = sem("counts_done")
        count_step = sem("count_step")
        ranks_done = sem("ranks_done")
        slot_ready = sem("slot_ready")
        tile_expert_ready = sem("tile_expert_ready")
        tile_turned = sem("tile_turned")
        tile_xT_ready = sem("tile_xT_ready")
        part_ready = sem("part_ready")
        final_ready = sem("final_ready")
        zeroed = sem("zeroed")
        consts_ready = sem("consts_ready")
        bv_ready = sem("bv_ready")
        tanh_ready = sem("tanh_ready")
        wo_turned = sem("wo_turned")
        woT_ready = sem("woT_ready")
        fused_done = sem("fused_done")
        fused_ready = sem("fused_ready")
        bias_ready = sem("bias_ready")
        ctx_turned = sem("ctx_turned")
        ctxT_ready = sem("ctxT_ready")
        stats_ready = sem("stats_ready")
        moments_ready = sem("moments_ready")
        var_ready = sem("var_ready")
        rstd_ready = sem("rstd_ready")
        xn_ready = sem("xn_ready")
        xn_turned = sem("xn_turned")
        xnT_ready = sem("xnT_ready")
        xb_ready = sem("xb_ready")
        vo_done = sem("vo_done")
        vo_ready = sem("vo_ready")
        g_done = sem("g_done")
        g_ready = sem("g_ready")
        scores_done = sem("scores_done")
        max_ready = sem("max_ready")
        neg_ready = sem("neg_ready")
        probs_ready = sem("probs_ready")
        inv_ready = sem("inv_ready")
        coef_ready = sem("coef_ready")
        probs_turned = sem("probs_turned")
        probsT_ready = sem("probsT_ready")
        pv_done = sem("pv_done")
        x2_ready = sem("x2_ready")
        x2n_ready = sem("x2n_ready")
        x2n_turned = sem("x2n_turned")
        x2nT_ready = sem("x2nT_ready")
        logits_done = sem("logits_done")
        sigmoid_ready = sem("sigmoid_ready")
        route_step = sem("route_step")
        gates_ready = sem("gates_ready")
        up_done = sem("up_done")
        silu_ready = sem("silu_ready")
        hid_ready = sem("hid_ready")
        down_done = sem("down_done")
        acc_ready = sem("acc_ready")
        r_up_done = sem("r_up_done")
        r_silu_ready = sem("r_silu_ready")
        r_hid_ready = sem("r_hid_ready")
        r_down_done = sem("r_down_done")
        tile_y_ready = sem("tile_y_ready")
        stored = sem("stored")

        block = stack.enter_context(nc.Block())
        x_dram = x.rearrange("b s d -> s b d")
        c_dram = ctx_in.rearrange("b s d -> s b d")
        o_dram = out.rearrange("b s d -> s b d")

        def halves(h):
            return slice(h * HALF, (h + 1) * HALF)

        @block.sync
        def _(sp):
            for h in range(2):
                sp.dma_start(ctx_sb[:, halves(h), :], c_dram[:, halves(h), :]).then_inc(ctx_loaded[h], 16)
                sp.dma_start(x_sb[:, halves(h), :], x_dram[:, halves(h), :]).then_inc(x_loaded[h], 16)
            sp.dma_start(w1s[:, :], shared_w1[0]).then_inc(shared_loaded, 16)
            sp.dma_start(w2s[:, :], shared_w2[0]).then_inc(shared_loaded, 16)
            sp.dma_start(w3s[:, :, :], shared_w3[0].rearrange("(j h) d -> h j d", h=P)).then_inc(shared_loaded, 16)
            sp.wait_ge(tile_expert_ready, 1)
            for j in range(TILES):
                e = sp.value_load(tile_expert[0:1, j:j + 1], min_val=0, max_val=E - 1)
                sp.dma_start(tile_w[:, j, :], routed_w[bass.ds(e, 1), :, :].rearrange("e p f -> (e p) f"))\
                  .then_inc(tile_w_loaded[j], 16)
            for q in range(B // 2):
                sp.wait_ge(final_ready, 2 * q + 2)
                sp.dma_start(o_dram[:, 2 * q:2 * q + 2, :], final[:, 2 * q:2 * q + 2, :]).then_inc(stored, 16)
            sp.wait_ge(stored, 16 * (B // 2))

        @block.gpsimd
        def _(pool):
            pool.dma_start(gains[:, 0:1], g_xattn.rearrange("(a n) -> a n", a=1).to_broadcast([P, 1])).then_inc(gains_loaded, 16)
            pool.dma_start(gains[:, 1:2], g_ffn.rearrange("(a n) -> a n", a=1).to_broadcast([P, 1])).then_inc(gains_loaded, 16)
            pool.dma_start(rw_sb[:, :], router_w).then_inc(router_loaded, 16)
            pool.dma_start(ebias[:, :], expert_bias.rearrange("(a n) -> a n", a=1).to_broadcast([P, E])).then_inc(router_loaded, 16)
            pool.memset(ident[:, :], 0.0).then_inc(zeroed, 1)
            pool.memset(ones_row[:, :], 1.0).then_inc(consts_ready, 1)
            pool.memset(ones_mat[:, :], 1.0).then_inc(consts_ready, 1)
            pool.memset(neg_half[:, :], -0.5).then_inc(consts_ready, 1)
            pool.iota(rev_index[:, :], pattern=[[-1, E]], base=E, channel_multiplier=0,
                      allow_small_or_imprecise_dtypes=True).then_inc(consts_ready, 1)
            pool.memset(zeros[:, :], 0.0).then_inc(zeroed, 1)
            pool.memset(ones_bf[:, :], 1.0).then_inc(consts_ready, 1)
            pool.memset(earlier_token[:, :], 1.0).then_inc(zeroed, 1)
            pool.memset(expert_order[:, :, :], 1.0).then_inc(zeroed, 1)
            pool.iota(tile_start[:, :], pattern=[[P, TILES]], base=0, channel_multiplier=0,
                      allow_small_or_imprecise_dtypes=True).then_inc(consts_ready, 1)
            pool.wait_ge(zeroed, 4)
            pool.affine_select(out=earlier_token[:, :], in_=earlier_token[:, :], compare_op=ALU.is_gt, fill=0.0,
                               base=0, pattern=[[1, P]], channel_multiplier=-1).then_inc(consts_ready, 1)
            pool.affine_select(out=expert_order[:, :, :], in_=expert_order[:, :, :], compare_op=ALU.is_gt, fill=0.0,
                               base=0, pattern=[[1, 2], [1, E]], channel_multiplier=-1).then_inc(consts_ready, 1)
            pool.dma_start(sorted_x.rearrange("(j p) d -> p j d", p=P), zeros[:, None, :].to_broadcast([P, TILES, D]))\
                .then_inc(rows_zeroed, 16)
            pool.affine_select(out=ident[:, :], in_=ident[:, :], compare_op=ALU.not_equal, fill=1.0,
                               base=0, pattern=[[-1, P]], channel_multiplier=1).then_inc(consts_ready, 1)
            for n in range(2):
                for h in range(2):
                    k = 2 * n + h
                    pool.wait_ge(moments_ready, HALF * (k + 1))
                    pool.tensor_scalar(var_eps[:, n, halves(h)], mean_var[:, n, halves(h), 1], EPS, None, ALU.add)\
                        .then_inc(var_ready, 1)
                    pool.wait_ge(var_ready, k + 1)
                    pool.wait_ge(consts_ready, CONSTS)
                    pool.tensor_tensor(rstd[:, n, halves(h)], var_eps[:, n, halves(h)], neg_half[:, :], ALU.pow)\
                        .then_inc(rstd_ready, 1)
                if n == 0:
                    pool.wait_ge(bias_ready, 1)
                    for h in range(2):
                        pool.wait_ge(x_loaded[h], 16)
                        pool.tensor_tensor(xb[:, halves(h), :], x_sb[:, halves(h), :],
                                           out_bias[:, None, :].to_broadcast([P, HALF, D]), ALU.add)\
                            .then_inc(xb_ready, 1)

            pool.wait_ge(rows_zeroed, 16)
            pool.wait_ge(slot_ready, 1)
            for b in range(B):
                pool.wait_ge(x2n_ready, b + 1)
                for k in range(TOP):
                    pool.indirect_dma_start(sorted_x[:, :], bass.IndirectOffsetOnAxis(slot[:, k * B + b:k * B + b + 1], 0),
                                            x2n[:, b, :], None).then_inc(rows_scattered, 16)
            for g in range(GROUPS):
                lo, hi = GROUP * g, min(GROUP * (g + 1), TILES)
                pool.wait_ge(tile_y_ready, g + 1)
                pool.dma_start(sorted_y.rearrange("(j p) d -> p j d", p=P)[:, lo:hi, :], tile_y[:, lo:hi, :])\
                    .then_inc(y_stored, 16)
            pool.wait_ge(y_stored, 16 * GROUPS)
            for b in range(B):
                for k in range(TOP):
                    pool.indirect_dma_start(picked_y[:, k * B + b, :], None, sorted_y[:, :],
                                            bass.IndirectOffsetOnAxis(slot[:, k * B + b:k * B + b + 1], 0))\
                        .then_inc(y_gathered[b], 16)

        @block.scalar
        def _(act):
            act.dma_start(wo_sb[:, :], Wo).then_inc(w_loaded, 16)
            act.dma_start(wq_sb[:, :], Wq).then_inc(w_loaded, 16)
            act.dma_start(wk_sb[:, :], Wk).then_inc(w_loaded, 16)
            act.dma_start(wv_sb[:, :], Wv).then_inc(w_loaded, 16)
            act.dma_start(bq_col[:, :], bq.rearrange("(p a) -> p a", a=1)).then_inc(small_loaded, 16)
            act.dma_start(bv_col[:, :], bv.rearrange("(p a) -> p a", a=1)).then_inc(small_loaded, 16)
            act.dma_start(bo_row[:, :], bo.rearrange("(a n) -> a n", a=1)).then_inc(small_loaded, 16)
            act.wait_ge(gains_loaded, 32)
            nc.scalar.activation(tanh_g[:, :], gains[:, :], ACT.Tanh).then_inc(tanh_ready, 1)
            act.wait_ge(wo_turned, 1)
            nc.scalar.copy(woT[:, :], bank[0][:, 0:128]).then_inc(woT_ready, 1)
            act.wait_ge(fused_done, 1)
            nc.scalar.copy(qk_w[:, :], bank[1][:, 0:128]).then_inc(fused_ready, 1)
            nc.scalar.copy(u_col[:, :], bank[1][:, 128:129]).then_inc(fused_ready, 1)
            act.wait_ge(fused_done, 2)
            nc.scalar.copy(vo_w[:, :], bank[0][:, 128:256]).then_inc(fused_ready, 1)
            act.wait_ge(tanh_ready, 1)
            nc.scalar.mul(out_bias[:, :], bank[0][:, 256:384], tanh_g[:, 0:1]).then_inc(bias_ready, 1)
            for h in range(2):
                act.wait_ge(ctx_turned, h + 1)
                nc.scalar.copy(ctxT[:, halves(h), :], bank[2 + h][:, :].rearrange("p (b s) -> p b s", b=HALF)).then_inc(ctxT_ready, 1)
            for h in range(2):
                act.wait_ge(xn_turned, h + 1)
                nc.scalar.copy(xnT[:, halves(h), :], bank[4 + h][:, :].rearrange("p (b s) -> p b s", b=HALF)).then_inc(xnT_ready, 1)
            for h in range(2):
                act.wait_ge(vo_done, h + 1)
                nc.scalar.copy(vo[:, halves(h), :], bank[6 + h][:, :].rearrange("p (b s) -> p b s", b=HALF)).then_inc(vo_ready, 1)
            for h in range(2):
                act.wait_ge(neg_ready, h + 1)
                for b in range(HALF):
                    k = HALF * h + b
                    nc.scalar.activation(probs[:, k, :], bank[2 + h][:, b * S:(b + 1) * S], ACT.Exp,
                                         bias=neg_max[:, k:k + 1], scale=SCALE,
                                         accum_out=row_sum[:, k:k + 1]).then_inc(probs_ready, 1)
            for h in range(2):
                act.wait_ge(x2n_turned, h + 1)
                nc.scalar.copy(x2nT[:, halves(h), :], bank[h][:, :].rearrange("p (b s) -> p b s", b=HALF)).then_inc(x2nT_ready, 1)
            act.wait_ge(logits_done, 1)
            nc.scalar.activation(scores[:, :, :], bank[2][:, 0:B * E].rearrange("p (b e) -> p b e", b=B), ACT.Sigmoid)\
                .then_inc(sigmoid_ready, 1)
            for k in range(2 * HJ):
                act.wait_ge(up_done, k + 1)
                if k >= 2:
                    act.wait_ge(hid_ready, k - 1)
                nc.scalar.activation(silu_t[:, k % 2, :], bank[4 + 2 * (k % 2)][:, :], ACT.Silu).then_inc(silu_ready, 1)
            act.wait_ge(rows_scattered, 16 * TOP * B)
            for g in range(GROUPS):
                lo, hi = GROUP * g, min(GROUP * (g + 1), TILES)
                act.dma_start(tile_x[:, lo:hi, :], sorted_x.rearrange("(j p) d -> p j d", p=P)[:, lo:hi, :])\
                    .then_inc(tile_x_loaded[g], 16)
            def turned(g):
                act.wait_ge(tile_turned, g + 1)
                n = P * (min(GROUP * (g + 1), TILES) - GROUP * g)
                nc.scalar.copy(tile_xT[:, g, 0:n], bank[2 + g % 2][:, 0:n]).then_inc(tile_xT_ready, 1)

            turned(0)
            turned(1)
            for j in range(TILES):
                act.wait_ge(r_up_done, j + 1)
                if j >= 2:
                    act.wait_ge(r_hid_ready, j - 1)
                nc.scalar.activation(tile_silu[:, j % 2, :], bank[4 + j % UP_RING][:, 0:P], ACT.Silu).then_inc(r_silu_ready, 1)
                if j % GROUP == 1 and j // GROUP + 2 < GROUPS:
                    turned(j // GROUP + 2)

        @block.vector
        def _(dve):
            def moments(n, src, h):
                for b in range(HALF):
                    k = HALF * h + b
                    nc.vector.bn_stats(stats[:, n, k, :], src[:, k, :]).then_inc(stats_ready, 1)
                for b in range(HALF):
                    k = HALF * h + b
                    dve.wait_ge(stats_ready, B * n + k + 1)
                    nc.vector.bn_aggr(mean_var[:, n, k, :], stats[:, n, k, :]).then_inc(moments_ready, 1)

            def normalise(n, src, dst, h, ready):
                dve.wait_ge(rstd_ready, 2 * n + h + 1)
                for b in range(HALF):
                    k = HALF * h + b
                    nc.vector.tensor_scalar(dst[:, k, :], src[:, k, :], mean_var[:, n, k, 0:1], rstd[:, n, k:k + 1],
                                            ALU.subtract, ALU.mult).then_inc(ready, 1)

            for h in range(2):
                dve.wait_ge(x_loaded[h], 16)
                moments(0, x_sb, h)
            dve.wait_ge(small_loaded, 48)
            dve.wait_ge(consts_ready, CONSTS)
            nc.vector.tensor_scalar(bv_mat[:, :], ones_mat[:, :], bv_col[:, 0:1], None, ALU.mult).then_inc(bv_ready, 1)
            for h in range(2):
                dve.wait_ge(moments_ready, B)
                normalise(0, x_sb, xn, h, xn_ready)
            for h in range(2):
                dve.wait_ge(g_done, h + 1)
                dve.wait_ge(fused_ready, 3)
                nc.vector.tensor_scalar(gT[:, halves(h), :], bank[h][:, :].rearrange("p (b s) -> p b s", b=HALF),
                                        u_col[:, 0:1], None, ALU.add).then_inc(g_ready, 1)
            for h in range(2):
                dve.wait_ge(scores_done, h + 1)
                nc.vector.reduce_max(row_max[:, halves(h)], bank[2 + h][:, :].rearrange("p (b s) -> p b s", b=HALF), AX)\
                    .then_inc(max_ready, 1)
                dve.wait_ge(max_ready, h + 1)
                nc.vector.tensor_scalar(neg_max[:, halves(h)], row_max[:, halves(h)], -SCALE, None, ALU.mult).then_inc(neg_ready, 1)
            for h in range(2):
                dve.wait_ge(probs_ready, HALF * (h + 1))
                nc.vector.reciprocal(inv_sum[:, halves(h)], row_sum[:, halves(h)]).then_inc(inv_ready, 1)
                dve.wait_ge(tanh_ready, 1)
                dve.wait_ge(inv_ready, h + 1)
                nc.vector.tensor_scalar(coef[:, halves(h)], inv_sum[:, halves(h)], tanh_g[:, 0:1], None, ALU.mult).then_inc(coef_ready, 1)
                dve.wait_ge(probs_turned, h + 1)
                nc.vector.tensor_copy(probsT[:, halves(h), :], bank[4 + h][:, :].rearrange("p (b s) -> p b s", b=HALF)).then_inc(probsT_ready, 1)
            for h in range(2):
                dve.wait_ge(pv_done, h + 1)
                dve.wait_ge(coef_ready, h + 1)
                dve.wait_ge(xb_ready, h + 1)
                for b in range(HALF):
                    k = HALF * h + b
                    nc.vector.scalar_tensor_tensor(x2[:, k, :], bank[6 + h][:, b * D:(b + 1) * D], coef[:, k:k + 1],
                                                   xb[:, k, :], ALU.mult, ALU.add).then_inc(x2_ready, 1)
                dve.wait_ge(x2_ready, HALF * (h + 1))
                moments(1, x2, h)
            dve.wait_ge(moments_ready, 2 * B)
            for h in range(2):
                normalise(1, x2, x2n, h, x2n_ready)

            steps = [0]

            def step(ins):
                ins.then_inc(route_step, 1)
                steps[0] += 1
                dve.wait_ge(route_step, steps[0])

            def per_expert(a):
                return a[:, :, None].to_broadcast([P, B, E])

            idx = rev_index[:, None, :].to_broadcast([P, B, E])
            dve.wait_ge(sigmoid_ready, 1)
            dve.wait_ge(router_loaded, 32)
            step(nc.vector.tensor_tensor(sel[:, 0], scores[:, :, :], ebias[:, None, :].to_broadcast([P, B, E]), ALU.add))
            for k in range(2):
                step(nc.vector.reduce_max(best[:, k], sel[:, k], AX))
                step(nc.vector.tensor_tensor(is_best[:, k], sel[:, k], per_expert(best[:, k]), ALU.is_equal))
                step(nc.vector.tensor_tensor(rank_of[:, k], is_best[:, k], idx, ALU.mult))
                step(nc.vector.reduce_max(first[:, k], rank_of[:, k], AX))
                step(nc.vector.tensor_tensor(onehot[:, k], idx, per_expert(first[:, k]), ALU.is_equal))
                if k == 0:
                    step(nc.vector.scalar_tensor_tensor(sel[:, 1], onehot[:, 0], -BIG, sel[:, 0], ALU.mult, ALU.add))
            nc.vector.tensor_tensor(chosen[:, :, :], onehot[:, 0], onehot[:, 1], ALU.add).then_inc(chosen_ready, 1)

            def slots():
                dve.wait_ge(counts_done, 1)
                nc.vector.tensor_scalar(raised_count[:, :], bank[2][0:E, 128:256], float(P - 1), None, ALU.add).then_inc(count_step, 1)
                dve.wait_ge(count_step, 1)
                nc.vector.tensor_scalar(tile_count[:, :], raised_count[:, :], P.bit_length() - 1, None, ALU.arith_shift_right)\
                    .then_inc(count_step, 1)
                dve.wait_ge(count_step, 2)
                nc.vector.tensor_scalar(padded_count[:, :], tile_count[:, :], float(P), None, ALU.mult).then_inc(count_step, 1)
                dve.wait_ge(ranks_done, 1)
                step(nc.vector.tensor_tensor(picked_rank[:, :, :].rearrange("p (k b) e -> p k (b e)", k=TOP),
                                             onehot[:, :, :, :].rearrange("p k b e -> p k (b e)"),
                                             bank[3][:, None, 0:B * E].to_broadcast([P, TOP, B * E]), ALU.mult))
                step(nc.vector.reduce_sum(slot_f[:, :], picked_rank[:, :, :], AX))
                nc.vector.tensor_copy(slot[:, :], slot_f[:, :]).then_inc(slot_ready, 1)
                step(nc.vector.tensor_tensor(passed[:, :, :], bank[2][0:1, None, 256 + E:256 + 2 * E].to_broadcast([1, TILES, E]),
                                             tile_start[:, :, None].to_broadcast([1, TILES, E]), ALU.is_le))
                step(nc.vector.reduce_sum(tile_expert_f[:, :], passed[:, :, :], AX))
                nc.vector.tensor_scalar(tile_expert[:, :], tile_expert_f[:, :], float(E - 1), None, ALU.min).then_inc(tile_expert_ready, 1)

            def make_gates():
                step(nc.vector.tensor_tensor(picked_score[:, :, :, :].rearrange("p k b e -> p k (b e)"),
                                             onehot[:, :, :, :].rearrange("p k b e -> p k (b e)"),
                                             scores[:, :, :].rearrange("p b e -> p (b e)")[:, None, :].to_broadcast([P, TOP, B * E]), ALU.mult))
                step(nc.vector.reduce_sum(gate_raw[:, :], picked_score[:, :, :, :].rearrange("p k b e -> p (k b) e"), AX))
                nc.vector.tensor_scalar(gates[:, :], gate_raw[:, :], tanh_g[:, 1:2], None, ALU.mult).then_inc(gates_ready, 1)

            slots()
            make_gates()
            for t in range(2):
                for j in range(HJ):
                    k = HJ * t + j
                    dve.wait_ge(silu_ready, k + 1)
                    if t == 1:
                        dve.wait_ge(down_done, 1)
                    nc.vector.tensor_tensor(hid[:, j, :], silu_t[:, k % 2, :], bank[5 + 2 * (k % 2)][:, :], ALU.mult)\
                        .then_inc(hid_ready, 1)
                dve.wait_ge(down_done, t + 1)
                nc.vector.scalar_tensor_tensor(acc[:, halves(t), :], bank[t][:, :].rearrange("p (b s) -> p b s", b=HALF), tanh_g[:, 1:2],
                                               x2[:, halves(t), :], ALU.mult, ALU.add).then_inc(acc_ready, 1)
            def evacuate(g):
                n = P * (min(GROUP * (g + 1), TILES) - GROUP * g)
                dve.wait_ge(r_down_done, min(GROUP * (g + 1), TILES))
                nc.vector.tensor_copy(tile_y[:, GROUP * g:GROUP * g + n // P, :].rearrange("p j d -> p (j d)"),
                                      bank[g % 2][:, 0:n]).then_inc(tile_y_ready, 1)

            for j in range(TILES):
                dve.wait_ge(r_silu_ready, j + 1)
                if j >= 3:
                    dve.wait_ge(r_down_done, j - 2)
                nc.vector.tensor_tensor(tile_hid[:, j % 3, :], tile_silu[:, j % 2, :], bank[4 + j % UP_RING][:, P:2 * P], ALU.mult)\
                    .then_inc(r_hid_ready, 1)
                if j % GROUP == 2 and j > GROUP:
                    evacuate(j // GROUP - 1)
            evacuate(GROUPS - 1)
            dve.wait_ge(gates_ready, 1)
            dve.wait_ge(acc_ready, 2)
            for b in range(B):
                dve.wait_ge(y_gathered[b], 32)
                nc.vector.scalar_tensor_tensor(part[:, b, :], picked_y[:, b, :], gates[:, b:b + 1], acc[:, b, :],
                                               ALU.mult, ALU.add).then_inc(part_ready, 1)
                dve.wait_ge(part_ready, b + 1)
                nc.vector.scalar_tensor_tensor(final[:, b, :], picked_y[:, B + b, :], gates[:, B + b:B + b + 1], part[:, b, :],
                                               ALU.mult, ALU.add).then_inc(final_ready, 1)

        @block.tensor
        def _(pe):
            pe.wait_ge(consts_ready, CONSTS)
            pe.wait_ge(w_loaded, 64)
            pe.wait_ge(small_loaded, 48)
            nc.tensor.transpose(bank[0][:, 0:128], wo_sb[:, :], ident[:, :]).then_inc(wo_turned, 1)
            nc.tensor.matmul(bank[1][:, 0:128], wq_sb[:, :], wk_sb[:, :], start=True, stop=True)
            nc.tensor.matmul(bank[1][:, 128:129], wk_sb[:, :], bq_col[:, :], start=True, stop=True).then_inc(fused_done, 1)
            pe.wait_ge(woT_ready, 1)
            nc.tensor.matmul(bank[0][:, 128:256], wv_sb[:, :], woT[:, :], start=True, stop=True)
            pe.wait_ge(bv_ready, 1)
            nc.tensor.matmul(bank[0][:, 256:384], bv_mat[:, :], woT[:, :], start=True, stop=False)
            nc.tensor.matmul(bank[0][:, 256:384], ones_row[:, :], bo_row[:, :], start=False, stop=True).then_inc(fused_done, 1)

            def turn(dst, src, h, done):
                for b in range(HALF):
                    last = nc.tensor.transpose(dst[:, b * P:(b + 1) * P], src[:, HALF * h + b, :], ident[:, :])
                last.then_inc(done, 1)

            for h in range(2):
                pe.wait_ge(ctx_loaded[h], 16)
                turn(bank[2 + h], ctx_sb, h, ctx_turned)
            for h in range(2):
                pe.wait_ge(xn_ready, HALF * (h + 1))
                turn(bank[4 + h], xn, h, xn_turned)
            pe.wait_ge(fused_ready, 3)
            pe.wait_ge(bias_ready, 1)
            for h in range(2):
                pe.wait_ge(ctxT_ready, h + 1)
                for b in range(HALF):
                    last = nc.tensor.matmul(bank[6 + h][:, b * P:(b + 1) * P], ctxT[:, HALF * h + b, :], vo_w[:, :], start=True, stop=True)
                last.then_inc(vo_done, 1)
            for h in range(2):
                pe.wait_ge(xnT_ready, h + 1)
                nc.tensor.matmul(bank[h][:, :], qk_w[:, :], xnT[:, halves(h), :], start=True, stop=True).then_inc(g_done, 1)
            for h in range(2):
                pe.wait_ge(g_ready, h + 1)
                for b in range(HALF):
                    k = HALF * h + b
                    last = nc.tensor.matmul(bank[2 + h][:, b * P:(b + 1) * P], gT[:, k, :], ctxT[:, k, :], start=True, stop=True)
                last.then_inc(scores_done, 1)
            for h in range(2):
                pe.wait_ge(probs_ready, HALF * (h + 1))
                turn(bank[4 + h], probs, h, probs_turned)
            for h in range(2):
                pe.wait_ge(probsT_ready, h + 1)
                pe.wait_ge(vo_ready, h + 1)
                for b in range(HALF):
                    k = HALF * h + b
                    last = nc.tensor.matmul(bank[6 + h][:, b * P:(b + 1) * P], probsT[:, k, :], vo[:, k, :], start=True, stop=True)
                last.then_inc(pv_done, 1)
            for h in range(2):
                pe.wait_ge(x2n_ready, HALF * (h + 1))
                turn(bank[h], x2n, h, x2n_turned)
            pe.wait_ge(x2nT_ready, 2)
            pe.wait_ge(router_loaded, 32)
            for k in range(B):
                last = nc.tensor.matmul(bank[2][:, k * E:(k + 1) * E], x2nT[:, k, :], rw_sb[:, :], start=True, stop=True)
            last.then_inc(logits_done, 1)

            def count():
                pe.wait_ge(chosen_ready, 1)
                for b in range(B):
                    last = nc.tensor.matmul(bank[2][0:E, 128:256], chosen[:, b, :], ones_bf[:, :], start=(b == 0), stop=(b == B - 1))
                last.then_inc(counts_done, 1)
                nc.tensor.matmul(bank[3][:, 0:B * E], earlier_token[:, :], chosen[:, :, :], start=True, stop=False, skip_group_check=True)
                for b in range(B - 1):
                    nc.tensor.matmul(bank[3][:, (b + 1) * E:B * E], ones_bf[:, :],
                                     chosen[:, b:b + 1, :].to_broadcast([P, B - 1 - b, E]), start=False, stop=False,
                                     skip_group_check=True)

            def rank():
                pe.wait_ge(count_step, 3)
                nc.tensor.matmul(bank[3][:, 0:B * E].rearrange("p (b e) -> p b e", b=B), padded_count[:, :],
                                 expert_order[:, 0:1, :].to_broadcast([E, B, E]), start=False, stop=True, skip_group_check=True)
                nc.tensor.matmul(bank[2][:, 256:256 + 2 * E], padded_count[:, :], expert_order[:, :, :].rearrange("p a e -> p (a e)"),
                                 start=True, stop=True).then_inc(ranks_done, 1)

            count()
            rank()
            pe.wait_ge(shared_loaded, 48)
            for t in range(2):
                for j in range(HJ):
                    k = HJ * t + j
                    if k >= 2:
                        pe.wait_ge(hid_ready, k - 1)
                    a = bank[4 + 2 * (k % 2)]
                    u = bank[5 + 2 * (k % 2)]
                    xt = x2nT[:, halves(t), :]
                    nc.tensor.matmul(a[:, :], w1s[:, j * P:(j + 1) * P], xt, start=True, stop=True)
                    nc.tensor.matmul(u[:, :], w2s[:, j * P:(j + 1) * P], xt, start=True, stop=True).then_inc(up_done, 1)
                pe.wait_ge(hid_ready, HJ * (t + 1))
                for b in range(HALF):
                    for j in range(HJ):
                        last = nc.tensor.matmul(bank[t][:, b * P:(b + 1) * P], hid[:, j, b * P:(b + 1) * P], w3s[:, j, :],
                                                start=(j == 0), stop=(j == HJ - 1))
                last.then_inc(down_done, 1)
            def turn_tiles(g):
                lo, hi = GROUP * g, min(GROUP * (g + 1), TILES)
                pe.wait_ge(tile_x_loaded[g], 16)
                if g >= 2:
                    pe.wait_ge(tile_xT_ready, g - 1)
                for j in range(lo, hi):
                    last = nc.tensor.transpose(bank[2 + g % 2][:, (j - lo) * P:(j - lo + 1) * P], tile_x[:, j, :], ident[:, :])
                last.then_inc(tile_turned, 1)

            def up(j):
                pe.wait_ge(tile_w_loaded[j], 16)
                pe.wait_ge(tile_xT_ready, j // GROUP + 1)
                if j >= UP_RING:
                    pe.wait_ge(r_hid_ready, j - UP_RING + 1)
                xt = tile_xT[:, j // GROUP, (j % GROUP) * P:(j % GROUP + 1) * P]
                dst = bank[4 + j % UP_RING]
                nc.tensor.matmul(dst[:, 0:P], tile_w[:, j, 0:P], xt, start=True, stop=True)
                nc.tensor.matmul(dst[:, P:2 * P], tile_w[:, j, P:2 * P], xt, start=True, stop=True).then_inc(r_up_done, 1)

            def down(j):
                g = j // GROUP
                pe.wait_ge(r_hid_ready, j + 1)
                if j % GROUP == 0 and g >= 2:
                    pe.wait_ge(tile_y_ready, g - 1)
                nc.tensor.matmul(bank[g % 2][:, (j % GROUP) * P:(j % GROUP + 1) * P], tile_hid[:, j % 3, :],
                                 tile_w[:, j, 2 * P:3 * P], start=True, stop=True).then_inc(r_down_done, 1)

            turn_tiles(0)
            turn_tiles(1)
            pe.wait_ge(acc_ready, 2)
            for j in range(TILES):
                up(j)
                if j % GROUP == 2 and j // GROUP + 2 < GROUPS:
                    turn_tiles(j // GROUP + 2)
                if j >= 2:
                    down(j - 2)
            down(TILES - 2)
            down(TILES - 1)


_INS = ['x', 'ctx_1024', 'g_xattn', 'g_ffn', 'L0_xattn_Wk', 'L0_xattn_Wv', 'L0_xattn_bv', 'L0_xattn_Wq',
        'L0_xattn_bq', 'L0_xattn_Wo', 'L0_xattn_bo', 'L0_ffn_router_w', 'L0_ffn_expert_bias', 'L0_ffn_shared_w1',
        'L0_ffn_shared_w2', 'L0_ffn_shared_w3']


def kernel(**inputs):
    import numpy as _np
    import concourse.bacc as _bacc
    from concourse import mybir as _mybir
    from concourse.bass_utils import run_bass_kernel_spmd as _run

    nc = _bacc.Bacc("TRN2", target_bir_lowering=False, num_devices=1)
    arrays, args = {}, []
    for name in _INS:
        a = _np.ascontiguousarray(inputs[name])
        arrays[f"in_{name}_dram"] = a
        args.append(nc.dram_tensor(f"in_{name}_dram", a.shape, _mybir.dt.from_np(a.dtype), kind="ExternalInput").ap())
    a = _np.concatenate([_np.asarray(inputs[f"L0_ffn_routed_w{m}"]) for m in (1, 2, 3)], axis=2)
    arrays["in_routed_w_dram"] = a
    args.append(nc.dram_tensor("in_routed_w_dram", a.shape, _mybir.dt.float32, kind="ExternalInput").ap())
    shape = inputs["x"].shape
    args.append(nc.dram_tensor("out_0_dram", shape, _mybir.dt.float32, kind="ExternalOutput").ap())
    flamingo_block(nc, *args)
    r = _run(nc, [arrays], core_ids=[0])
    return r.results[0]["out_0_dram"]
```

```python
from contextlib import ExitStack

import concourse.bass as bass
from concourse import mybir

F32 = mybir.dt.float32
BF16 = mybir.dt.bfloat16
I32 = mybir.dt.int32
U32 = mybir.dt.uint32
ALU = mybir.AluOpType
ACT = mybir.ActivationFunctionType
AX = mybir.AxisListType.X

P = 128



def flamingo_block(
    nc: bass.Bass,
    x: bass.AP,
    ctx_in: bass.AP,
    attn_params: bass.AP,
    row_params: bass.AP,
    shared_w: bass.AP,
    routed_w: bass.AP,
    out: bass.AP,
):
    B, S, D = x.shape
    E = routed_w.shape[0]
    H = shared_w.shape[1] // 3
    HJ = H // P
    HALF = B // 2
    SCALE = float(D) ** -0.5
    EPS = 1e-5
    TOP = 2
    RUNS = TOP * E
    TILES = TOP * (B * S // P + E - 1)
    ROUTE_CONSTS = 6
    ROUND = 1.5 * 2.0 ** (23 + P.bit_length() - 1)
    GROUP = 2
    GROUPS = -(-TILES // GROUP)
    SURE = TOP * B * S // P // GROUP
    PAIR = 2
    PAIRS = -(-TILES // PAIR)
    EARLY = B * S // P
    WEIGHT_RING = 24
    PLACE_AHEAD = 4
    ROWS_RING = 16
    WEIGHTS_AHEAD = 14
    ROWS_FIRST = 3
    SHARED_EARLY = HJ + 2
    PV_BANK = (6, 2, 3, 7)
    ROW = D + 1
    UP_RING = 4
    assert S == P and D == P and HALF * P == 512

    with ExitStack() as stack:
        def sb(name, shape, dt=F32):
            return stack.enter_context(nc.sbuf_tensor(name, shape, dt))

        def sem(name):
            return stack.enter_context(nc.semaphore(name))

        bank = [stack.enter_context(nc.psum_tensor(f"bank{i}", [P, 512], F32)) for i in range(8)]

        x_sb = sb("x_sb", [P, B, D])
        ctx_sb = sb("ctx_sb", [P, B, D])
        params = sb("params", [P, 4 * D + 2 + E])
        wo_sb, wq_sb, wk_sb, wv_sb = (params[:, m * D:(m + 1) * D] for m in range(4))
        bq_col, bv_col = params[:, 4 * D:4 * D + 1], params[:, 4 * D + 1:4 * D + 2]
        rw_sb = params[:, 4 * D + 2:4 * D + 2 + E]
        rows = sb("rows", [P, D + E + 2])
        bo_row, ebias, gains = rows[0:1, 0:D], rows[:, D:D + E], rows[:, D + E:D + E + 2]
        shared_sb = sb("shared_sb", [P, 3 * H])
        w1s, w2s = shared_sb[:, 0:H], shared_sb[:, H:2 * H]
        w3s = shared_sb[:, 2 * H:3 * H].rearrange("p (j d) -> p j d", j=HJ)
        ident = sb("ident", [P, P])
        ones_row = sb("ones_row", [1, P])
        ones_mat = sb("ones_mat", [P, P])
        bv_mat = sb("bv_mat", [P, P])
        neg_half = sb("neg_half", [P, HALF])
        expert_index = sb("expert_index", [P, E])
        half_less = sb("half_less", [1, RUNS], BF16)
        ones_bf = sb("ones_bf", [P, P], BF16)
        earlier_token = sb("earlier_token", [P, P], BF16)
        run_order = sb("run_order", [RUNS, 2, RUNS], BF16)
        tile_start = sb("tile_start", [P, 1])
        woT = sb("woT", [P, D])
        qk_w = sb("qk_w", [P, D])
        vo_w = sb("vo_w", [P, D])
        u_col = sb("u_col", [P, 1])
        tanh_g = sb("tanh_g", [P, 2])
        vo_bias = sb("vo_bias", [P, D])
        stats = sb("stats", [P, 2, B, 6])
        mean_var = sb("mean_var", [P, 2, B, 2])
        var_eps = sb("var_eps", [P, 2, B])
        rstd = sb("rstd", [P, 2, B])
        xn = sb("xn", [P, B, D])
        ctxT = sb("ctxT", [P, B, S])
        xnT = sb("xnT", [P, B, S])
        gT = sb("gT", [P, B, S])
        vo = sb("vo", [P, B, D])
        row_max = sb("row_max", [P, B])
        neg_max = sb("neg_max", [P, B])
        probs = sb("probs", [P, B, S])
        row_sum = sb("row_sum", [P, B])
        inv_sum = sb("inv_sum", [P, B])
        probsT = sb("probsT", [P, B, S])
        last_part = sb("last_part", [P, 2, D])
        x2 = sb("x2", [P, B, D])
        x2n = sb("x2n", [P, TOP, B, ROW])
        x2T = sb("x2T", [P, B, S])
        x2nT = sb("x2nT", [P, B, S])
        shift = sb("shift", [P, B])
        router_c = sb("router_c", [P, E])
        logits = sb("logits", [P, B, E])
        scores = sb("scores", [P, B, E])
        sel = sb("sel", [P, B, E])
        top_values = sb("top_values", [P, B, 8])
        top_index = sb("top_index", [P, B, 8], U32)
        onehot = sb("onehot", [P, B, TOP, E], BF16)
        padded_count = sb("padded_count", [RUNS, 1], BF16)
        picked_rank = sb("picked_rank", [P, TOP * B, E])
        slot = sb("slot", [P, TOP * B], U32)
        passed = sb("passed", [TILES, RUNS])
        runs_before = sb("runs_before", [TILES, 1])
        tile_run = sb("tile_run", [TILES, 1])
        second_set = sb("second_set", [TILES, 1])
        tile_expert = sb("tile_expert", [TILES, 1], I32)
        tile_count = sb("tile_count", [1, 1], I32)
        picked_score = sb("picked_score", [P, B, TOP, E])
        gate_raw = sb("gate_raw", [P, TOP * B])
        gates = sb("gates", [P, TOP * B])
        silu_t = sb("silu_t", [P, 2, 512])
        hid = sb("hid", [P, HJ, 512])
        acc = sb("acc", [P, HALF, D])
        tile_w = sb("tile_w", [P, WEIGHT_RING, 3 * P])
        tile_x = sb("tile_x", [P, TILES, ROW])
        tile_place = sb("tile_place", [P, TILES], U32)
        tile_xT = sb("tile_xT", [P, 3, PAIR * P])
        tile_silu = sb("tile_silu", [P, 2, P])
        tile_hid = sb("tile_hid", [P, 3, P])
        tile_y = sb("tile_y", [P, TILES, D])
        picked_y = sb("picked_y", [P, TOP * B, D])
        gated = sb("gated", [P, B, D])
        second_gated = sb("second_gated", [P, 2, D])
        rest = sb("rest", [P, B, D])
        final = sb("final", [P, B, D])
        sorted_x = nc.dram_tensor("sorted_x", [TILES * P, ROW], F32).ap()
        placed_y = nc.dram_tensor("placed_y", [TOP * B * S + TILES * P, D], F32).ap()

        params_loaded = sem("params_loaded")
        rows_loaded = sem("rows_loaded")
        ctx_loaded = [sem(f"ctx_loaded{i}") for i in range(2)]
        x_loaded = [sem(f"x_loaded{i}") for i in range(2)]
        shared_loaded = sem("shared_loaded")
        rows_zeroed = sem("rows_zeroed")
        rows_scattered = [sem(f"rows_scattered{k}") for k in range(TOP)]
        tile_x_loaded = [sem(f"tile_x_loaded{i}") for i in range(ROWS_RING)]
        tile_w_loaded = [sem(f"tile_w_loaded{i}") for i in range(WEIGHT_RING)]
        y_placed = [sem(f"y_placed{i}") for i in range(2 * PLACE_AHEAD)]
        first_loaded = [sem(f"first_loaded{h}") for h in range(2)]
        rest_ready = sem("rest_ready")
        all_placed = sem("all_placed")
        y_loaded = [sem(f"y_loaded{q}") for q in range(B // 2)]
        onehot_ready = sem("onehot_ready")
        counts_done = sem("counts_done")
        padded_ready = sem("padded_ready")
        ranks_done = sem("ranks_done")
        ends_done = sem("ends_done")
        picked_rank_ready = sem("picked_rank_ready")
        slot_ready = sem("slot_ready")
        tile_expert_ready = sem("tile_expert_ready")
        tile_turned = sem("tile_turned")
        tile_xT_ready = sem("tile_xT_ready")
        first_final_ready = sem("first_final_ready")
        last_final_ready = sem("last_final_ready")
        zeroed = sem("zeroed")
        consts_ready = sem("consts_ready")
        ident_ready = sem("ident_ready")
        padding_cleared = sem("padding_cleared")
        padding_ready = sem("padding_ready")
        own_place_ready = sem("own_place_ready")
        copies_ready = sem("copies_ready")
        place_ready = sem("place_ready")
        gated_ready = sem("gated_ready")
        second_gated_ready = sem("second_gated_ready")
        route_consts_ready = sem("route_consts_ready")
        bv_ready = sem("bv_ready")
        tanh_ready = sem("tanh_ready")
        wo_turned = sem("wo_turned")
        woT_ready = sem("woT_ready")
        fused_done = sem("fused_done")
        fused_ready = sem("fused_ready")
        bias_ready = sem("bias_ready")
        vo_w_ready = sem("vo_w_ready")
        ctx_turned = sem("ctx_turned")
        ctxT_ready = sem("ctxT_ready")
        stats_ready = sem("stats_ready")
        moments_ready = sem("moments_ready")
        var_ready = sem("var_ready")
        rstd_ready = sem("rstd_ready")
        xn_ready = sem("xn_ready")
        xn_turned = sem("xn_turned")
        xnT_ready = sem("xnT_ready")
        probsT_ready_too = sem("probsT_ready_too")
        vo_done = sem("vo_done")
        vo_ready = sem("vo_ready")
        g_done = sem("g_done")
        g_ready = sem("g_ready")
        scores_done = sem("scores_done")
        max_ready = sem("max_ready")
        neg_ready = sem("neg_ready")
        probs_ready = sem("probs_ready")
        inv_ready = sem("inv_ready")
        probs_turned = sem("probs_turned")
        probsT_ready = sem("probsT_ready")
        pv_done = sem("pv_done")
        x2_ready = sem("x2_ready")
        last_part_ready = sem("last_part_ready")
        last_x2_ready = sem("last_x2_ready")
        x2_turned = sem("x2_turned")
        x2T_ready = sem("x2T_ready")
        router_sum_done = sem("router_sum_done")
        router_ready = sem("router_ready")
        logits_ready = sem("logits_ready")
        shift_ready = sem("shift_ready")
        x2n_ready = sem("x2n_ready")
        x2n_turned = sem("x2n_turned")
        x2nT_ready = sem("x2nT_ready")
        logits_done = sem("logits_done")
        sigmoid_ready = sem("sigmoid_ready")
        route_step = sem("route_step")
        gates_ready = sem("gates_ready")
        up_done = sem("up_done")
        silu_ready = sem("silu_ready")
        hid_ready = sem("hid_ready")
        down_done = sem("down_done")
        acc_ready = sem("acc_ready")
        r_up_done = sem("r_up_done")
        r_silu_ready = sem("r_silu_ready")
        r_hid_ready = sem("r_hid_ready")
        r_down_done = sem("r_down_done")
        tile_y_ready = sem("tile_y_ready")
        stored = sem("stored")

        block = stack.enter_context(nc.Block())
        x_dram = x.rearrange("b s d -> s b d")
        c_dram = ctx_in.rearrange("b s d -> s b d")
        o_dram = out.rearrange("b s d -> s b d")

        def halves(h):
            return slice(h * HALF, (h + 1) * HALF)

        def wait_placed(engine, start, stop):
            for j in range(start, stop):
                engine.wait_ge(y_placed[j % len(y_placed)], 16 * (j // len(y_placed) + 1))

        def twos(p):
            return slice(2 * p, 2 * p + 2)

        def tiles(g):
            return slice(GROUP * g, min(GROUP * (g + 1), TILES))

        def pair(p):
            return slice(PAIR * p, min(PAIR * (p + 1), TILES))

        def tiles_in_pair(p):
            return pair(p).stop - pair(p).start

        @block.sync
        def _(sp):
            for h in range(2):
                sp.dma_start(x_sb[:, halves(h), :], x_dram[:, halves(h), :]).then_inc(x_loaded[h], 16)
            sp.dma_start(ctx_sb[:, halves(1), :], c_dram[:, halves(1), :]).then_inc(ctx_loaded[1], 16)
            sp.dma_start(shared_sb[:, :], shared_w).then_inc(shared_loaded, 16)
            sp.wait_ge(padding_ready, 1)
            sp.dma_start(sorted_x.rearrange("(j p) d -> p j d", p=P), tile_x[:, :, :]).then_inc(rows_zeroed, 16)

            def load_weights(j):
                if j >= WEIGHT_RING:
                    sp.wait_ge(r_down_done, j - WEIGHT_RING + 1)
                e = sp.value_load(tile_expert[j:j + 1, 0:1], min_val=0, max_val=E - 1)
                sp.dma_start(tile_w[:, j % WEIGHT_RING, :], routed_w[bass.ds(e, 1), :, :].rearrange("e p f -> (e p) f"))\
                  .then_inc(tile_w_loaded[j % WEIGHT_RING], 16)

            def load_rows(p):
                sp.dma_start(tile_x[:, pair(p), :], sorted_x.rearrange("(j p) d -> p j d", p=P)[:, pair(p), :])\
                  .then_inc(tile_x_loaded[p % ROWS_RING], 16)

            def first_sets_placed(total):
                done = total - EARLY
                wait_placed(sp, max(done - len(y_placed), 0), done)

            def more_groups(g):
                if g < GROUPS:
                    with sp.If(count > GROUP * g):
                        for p in range(GROUP * g // PAIR + 1, min(GROUP * (g + 1) // PAIR + 1, PAIRS)):
                            load_rows(p)
                        for j in range(tiles(g).start, tiles(g).stop):
                            load_weights(j)
                        more_groups(g + 1)
                    with sp.Else():
                        first_sets_placed(GROUP * g)
                else:
                    first_sets_placed(TILES)

            sp.wait_ge(tile_expert_ready, 2)
            for j in range(WEIGHTS_AHEAD):
                load_weights(j)
            sp.wait_ge(rows_scattered[1], 16 * B)
            for p in range(EARLY // PAIR, EARLY // PAIR + ROWS_FIRST):
                load_rows(p)
            for j in range(WEIGHTS_AHEAD, GROUP * SURE):
                load_weights(j)
            for p in range(EARLY // PAIR + ROWS_FIRST, GROUP * SURE // PAIR + 1):
                load_rows(p)
            count = sp.value_load(tile_count[0:1, 0:1], min_val=GROUP * SURE, max_val=TILES)
            more_groups(SURE)
            placed = placed_y[0:TOP * B * S, :].rearrange("(b k s) d -> s b k d", k=TOP, s=S)
            picked = picked_y[:, :, :].rearrange("p (b k) d -> p b k d", k=TOP)
            for h in range(2):
                sp.dma_start(picked[:, halves(h), 0, :], placed[:, halves(h), 0, :]).then_inc(first_loaded[h], 16)
            sp.wait_ge(all_placed, 1)
            for q in range(B // 2):
                sp.dma_start(picked[:, twos(q), 1, :], placed[:, twos(q), 1, :]).then_inc(y_loaded[q], 16)
            for q in (1, 0, *range(2, B // 2)):
                if q == 0:
                    sp.wait_ge(first_final_ready, 1)
                else:
                    sp.wait_ge(last_final_ready, 2 * q)
                sp.dma_start(o_dram[:, twos(q), :], final[:, twos(q), :]).then_inc(stored, 16)
            sp.wait_ge(stored, 16 * (B // 2))

        @block.gpsimd
        def _(pool):
            pool.memset(ident[:, :], 0.0).then_inc(zeroed, 1)
            pool.wait_ge(zeroed, 1)
            pool.affine_select(out=ident[:, :], in_=ident[:, :], compare_op=ALU.not_equal, fill=1.0,
                               base=0, pattern=[[-1, P]], channel_multiplier=1).then_inc(ident_ready, 1)
            pool.memset(neg_half[:, :], -0.5).then_inc(consts_ready, 1)
            pool.memset(ones_mat[:, :], 1.0).then_inc(consts_ready, 1)
            pool.memset(ones_row[:, :], 1.0).then_inc(consts_ready, 1)
            pool.iota(x2n[:, :, :, D], pattern=[[S, TOP], [TOP * S, B]], base=0, channel_multiplier=1,
                      allow_small_or_imprecise_dtypes=True).then_inc(own_place_ready, 1)

            def inverse_deviation(n, h):
                pool.wait_ge(var_ready, 2 * n + h + 1)
                pool.tensor_tensor(rstd[:, n, halves(h)], var_eps[:, n, halves(h)], neg_half[:, :], ALU.pow)\
                    .then_inc(rstd_ready, 1)

            pool.wait_ge(consts_ready, 3)
            inverse_deviation(0, 0)
            inverse_deviation(0, 1)
            pool.memset(ones_bf[:, :], 1.0).then_inc(route_consts_ready, 1)
            pool.memset(half_less[:, :], 0.5 * (P - 1)).then_inc(route_consts_ready, 1)
            pool.iota(expert_index[:, :], pattern=[[1, E]], base=0, channel_multiplier=0,
                      allow_small_or_imprecise_dtypes=True).then_inc(route_consts_ready, 1)
            pool.iota(tile_start[:, :], pattern=[[0, 1]], base=0, channel_multiplier=P,
                      allow_small_or_imprecise_dtypes=True).then_inc(route_consts_ready, 1)
            pool.memset(earlier_token[:, :], 1.0).then_inc(zeroed, 1)
            pool.memset(run_order[:, :, :], 1.0).then_inc(zeroed, 1)
            pool.wait_ge(zeroed, 3)
            pool.affine_select(out=earlier_token[:, :], in_=earlier_token[:, :], compare_op=ALU.is_gt, fill=0.0,
                               base=0, pattern=[[1, P]], channel_multiplier=-1).then_inc(route_consts_ready, 1)
            pool.affine_select(out=run_order[:, :, :], in_=run_order[:, :, :], compare_op=ALU.is_gt, fill=0.0,
                               base=0, pattern=[[1, 2], [1, RUNS]], channel_multiplier=-1).then_inc(route_consts_ready, 1)
            pool.memset(tile_x[:, :, :], 0.0).then_inc(padding_cleared, 1)
            pool.wait_ge(padding_cleared, 1)
            pool.iota(tile_x[:, :, D], pattern=[[P, TILES]], base=TOP * B * S, channel_multiplier=1,
                      allow_small_or_imprecise_dtypes=True).then_inc(padding_ready, 1)
            pool.wait_ge(last_part_ready, 2)
            pool.wait_ge(x_loaded[1], 16)
            pool.tensor_tensor(x2[:, B - 2:B, :], last_part[:, :, :], x_sb[:, B - 2:B, :], ALU.add).then_inc(last_x2_ready, 1)
            inverse_deviation(1, 0)
            inverse_deviation(1, 1)
            pool.wait_ge(rows_zeroed, 16)
            pool.wait_ge(own_place_ready, 1)
            for k in range(TOP):
                pool.wait_ge(slot_ready, k + 1)
                for b in range(B):
                    if k == 0:
                        pool.wait_ge(x2n_ready, b + 1)
                    else:
                        pool.wait_ge(copies_ready, 1)
                    pool.indirect_dma_start(sorted_x[:, :], bass.IndirectOffsetOnAxis(slot[:, k * B + b:k * B + b + 1], 0),
                                            x2n[:, k, b, :], None).then_inc(rows_scattered[k], 16)
            pool.wait_ge(tile_expert_ready, 2)
            count = pool.value_load(tile_count[0:1, 0:1], min_val=GROUP * SURE, max_val=TILES)

            def place(j):
                if j >= PLACE_AHEAD:
                    wait_placed(pool, j - PLACE_AHEAD, j - PLACE_AHEAD + 1)
                pool.wait_ge(place_ready, j // PAIR + 1)
                pool.wait_ge(tile_y_ready, j + 1)
                pool.indirect_dma_start(placed_y[:, :], bass.IndirectOffsetOnAxis(tile_place[:, j:j + 1], 0),
                                        tile_y[:, j, :], None).then_inc(y_placed[j % len(y_placed)], 16)

            def more_tiles(j):
                if j < TILES:
                    with pool.If(count > j):
                        place(j)
                        more_tiles(j + 1)
                    with pool.Else():
                        wait_placed(pool, j - PLACE_AHEAD, j)
                else:
                    wait_placed(pool, TILES - PLACE_AHEAD, TILES)

            for j in range(GROUP * SURE):
                place(j)
            more_tiles(GROUP * SURE)
            pool.sem_inc(all_placed, 1)
            pool.wait_ge(rest_ready, 1)
            pool.wait_ge(second_gated_ready, 2)
            pool.tensor_tensor(final[:, twos(0), :], second_gated[:, :, :], rest[:, twos(0), :], ALU.add).then_inc(first_final_ready, 1)

        @block.scalar
        def _(act):
            act.dma_start(params[:, :], attn_params).then_inc(params_loaded, 16)
            act.dma_start(ctx_sb[:, halves(0), :], c_dram[:, halves(0), :]).then_inc(ctx_loaded[0], 16)
            act.dma_start(rows[:, :], row_params.to_broadcast([P, D + E + 2])).then_inc(rows_loaded, 16)
            nc.scalar.preload_act_table(ACT.Exp)
            act.wait_ge(wo_turned, 1)
            nc.scalar.copy(woT[:, :], bank[0][:, 0:128]).then_inc(woT_ready, 1)
            act.wait_ge(fused_done, 1)
            nc.scalar.copy(qk_w[:, :], bank[1][:, 0:128]).then_inc(fused_ready, 1)
            nc.scalar.copy(u_col[:, :], bank[1][:, 128:129]).then_inc(fused_ready, 1)
            act.wait_ge(rows_loaded, 16)
            nc.scalar.activation(tanh_g[:, :], gains, ACT.Tanh).then_inc(tanh_ready, 1)
            act.wait_ge(fused_done, 2)
            act.wait_ge(tanh_ready, 1)
            nc.scalar.mul(vo_w[:, :], bank[6][:, 0:128], tanh_g[:, 0:1]).then_inc(vo_w_ready, 1)
            for h in range(2):
                act.wait_ge(ctx_turned, h + 1)
                nc.scalar.copy(ctxT[:, halves(h), :], bank[2 + h][:, :].rearrange("p (b s) -> p b s", b=HALF)).then_inc(ctxT_ready, 1)
            for h in range(2):
                act.wait_ge(xn_turned, h + 1)
                nc.scalar.copy(xnT[:, halves(h), :], bank[4 + h][:, :].rearrange("p (b s) -> p b s", b=HALF)).then_inc(xnT_ready, 1)
            for h in range(2):
                act.wait_ge(g_done, h + 1)
                nc.scalar.activation(gT[:, halves(h), :], bank[h][:, :].rearrange("p (b s) -> p b s", b=HALF), ACT.Identity,
                                     bias=u_col[:, 0:1]).then_inc(g_ready, 1)
            act.wait_ge(fused_done, 3)
            nc.scalar.mul(vo_bias[:, :], bank[6][:, 128:256], tanh_g[:, 0:1]).then_inc(bias_ready, 1)
            for p in range(HALF):
                act.wait_ge(neg_ready, p + 1)
                for b in (2 * p, 2 * p + 1):
                    nc.scalar.activation(probs[:, b, :], bank[2 + p][:, (b % 2) * S:(b % 2 + 1) * S], ACT.Exp,
                                         bias=neg_max[:, b:b + 1], scale=SCALE,
                                         accum_out=row_sum[:, b:b + 1]).then_inc(probs_ready, 1)
            for p in range(1, HALF):
                act.wait_ge(probs_turned, p + 1)
                nc.scalar.copy(probsT[:, twos(p), :], bank[p % 2][:, 0:256].rearrange("p (b s) -> p b s", b=2))\
                    .then_inc(probsT_ready_too, 1)
            act.wait_ge(pv_done, HALF)
            act.wait_ge(inv_ready, 1)
            for b in range(2):
                nc.scalar.mul(last_part[:, b, :], bank[PV_BANK[3]][:, b * D:(b + 1) * D], inv_sum[:, B - 2 + b:B - 1 + b])\
                    .then_inc(last_part_ready, 1)
            nc.scalar.preload_act_table(ACT.Sigmoid)
            for h in range(2):
                act.wait_ge(x2_turned, h + 1)
                nc.scalar.copy(x2T[:, halves(h), :], bank[4 + h][:, :].rearrange("p (b s) -> p b s", b=HALF)).then_inc(x2T_ready, 1)
            act.wait_ge(logits_ready, 1)
            nc.scalar.activation(scores[:, :, :], logits[:, :, :], ACT.Sigmoid).then_inc(sigmoid_ready, 1)
            act.wait_ge(shift_ready, 1)

            def normalise(b):
                nc.scalar.activation(x2n[:, 0, b, 0:D], x2[:, b, :], ACT.Identity, bias=shift[:, b:b + 1],
                                     scale=rstd[:, 1, b:b + 1]).then_inc(x2n_ready, 1)

            def copy_turned(h):
                act.wait_ge(x2n_turned, h + 1)
                nc.scalar.copy(x2nT[:, halves(h), :], bank[h][:, :].rearrange("p (b s) -> p b s", b=HALF)).then_inc(x2nT_ready, 1)

            for b in range(B):
                normalise(b)
                if b == B - 3:
                    copy_turned(0)
            nc.scalar.preload_act_table(ACT.Silu)

            def share(k):
                act.wait_ge(up_done, k + 1)
                if k >= 2:
                    act.wait_ge(hid_ready, k - 1)
                nc.scalar.activation(silu_t[:, k % 2, :], bank[4 + 2 * (k % 2)][:, :], ACT.Silu).then_inc(silu_ready, 1)

            share(0)
            copy_turned(1)
            act.wait_ge(x2n_ready, B)
            nc.scalar.copy(x2n[:, 1, :, 0:D], x2n[:, 0, :, 0:D]).then_inc(copies_ready, 1)
            for k in range(1, HJ + 1):
                share(k)
            act.wait_ge(tile_expert_ready, 2)
            count = act.value_load(tile_count[0:1, 0:1], min_val=GROUP * SURE, max_val=TILES)
            act.wait_ge(rows_scattered[0], 16 * B)
            for p in range(EARLY // PAIR):
                act.dma_start(tile_x[:, pair(p), :], sorted_x.rearrange("(j p) d -> p j d", p=P)[:, pair(p), :])\
                    .then_inc(tile_x_loaded[p % ROWS_RING], 16)
            for k in range(HJ + 1, SHARED_EARLY):
                share(k)

            def turned(p):
                act.wait_ge(tile_turned, p + 1)
                n = P * tiles_in_pair(p)
                nc.scalar.copy(tile_xT[:, p % 3, 0:n], bank[2 + p % 2][:, 0:n]).then_inc(tile_xT_ready, 1)

            def group(g):
                for j in range(tiles(g).start, tiles(g).stop):
                    if j in (0, EARLY):
                        turned(j // PAIR)
                    act.wait_ge(r_up_done, j + 1)
                    if j >= 2:
                        act.wait_ge(r_hid_ready, j - 1)
                    nc.scalar.activation(tile_silu[:, j % 2, :], bank[4 + j % UP_RING][:, 0:P], ACT.Silu).then_inc(r_silu_ready, 1)
                    if j % PAIR == 0 and j + PAIR not in (EARLY, TILES):
                        turned(j // PAIR + 1)

            def more_groups(g):
                if g < GROUPS:
                    with act.If(count > GROUP * g):
                        group(g)
                        more_groups(g + 1)

            for g in range(SURE):
                group(g)
            more_groups(SURE)
            act.wait_ge(gates_ready, 1)
            for h in range(2):
                share(SHARED_EARLY + h)
                act.wait_ge(first_loaded[h], 16)
                for b in range(HALF * h, HALF * (h + 1)):
                    nc.scalar.mul(gated[:, b, :], picked_y[:, TOP * b, :], gates[:, TOP * b:TOP * b + 1]).then_inc(gated_ready, 1)
            for b in range(2):
                act.wait_ge(y_loaded[0], 16)
                nc.scalar.mul(second_gated[:, b, :], picked_y[:, TOP * b + 1, :], gates[:, TOP * b + 1:TOP * b + 2])\
                    .then_inc(second_gated_ready, 1)

        @block.vector
        def _(dve):
            def moments(n, src, h):
                for b in range(HALF):
                    k = HALF * h + b
                    nc.vector.bn_stats(stats[:, n, k, :], src[:, k, :]).then_inc(stats_ready, 1)
                for b in range(HALF):
                    k = HALF * h + b
                    dve.wait_ge(stats_ready, B * n + k + 1)
                    nc.vector.bn_aggr(mean_var[:, n, k, :], stats[:, n, k, :]).then_inc(moments_ready, 1)
                dve.wait_ge(moments_ready, B * n + HALF * (h + 1))
                nc.vector.tensor_scalar(var_eps[:, n, halves(h)], mean_var[:, n, halves(h), 1], EPS, None, ALU.add)\
                    .then_inc(var_ready, 1)

            def normalise(n, src, dst, h, ready):
                dve.wait_ge(rstd_ready, 2 * n + h + 1)
                for b in range(HALF):
                    k = HALF * h + b
                    nc.vector.tensor_scalar(dst[:, k, :], src[:, k, :], mean_var[:, n, k, 0:1], rstd[:, n, k:k + 1],
                                            ALU.subtract, ALU.mult).then_inc(ready, 1)

            dve.wait_ge(x_loaded[0], 16)
            moments(0, x_sb, 0)
            dve.wait_ge(params_loaded, 16)
            dve.wait_ge(consts_ready, 3)
            nc.vector.tensor_scalar(bv_mat[:, :], ones_mat[:, :], bv_col, None, ALU.mult).then_inc(bv_ready, 1)
            dve.wait_ge(x_loaded[1], 16)
            moments(0, x_sb, 1)
            dve.wait_ge(moments_ready, B)
            for h in range(2):
                normalise(0, x_sb, xn, h, xn_ready)
            dve.wait_ge(router_sum_done, 1)
            nc.vector.scalar_tensor_tensor(router_c[:, :], bank[7][:, 0:E], -1.0 / D, rw_sb, ALU.mult, ALU.add)\
                .then_inc(router_ready, 1)
            for p in range(HALF):
                dve.wait_ge(scores_done, p + 1)
                nc.vector.reduce_max(row_max[:, twos(p)], bank[2 + p][:, 0:256].rearrange("p (b s) -> p b s", b=2), AX)\
                    .then_inc(max_ready, 1)
                dve.wait_ge(max_ready, p + 1)
                nc.vector.tensor_scalar(neg_max[:, twos(p)], row_max[:, twos(p)], -SCALE, None, ALU.mult).then_inc(neg_ready, 1)

            def add_bias(h):
                dve.wait_ge(vo_done, h + 1)
                dve.wait_ge(bias_ready, 1)
                nc.vector.tensor_tensor(vo[:, halves(h), :], bank[6 + h][:, :].rearrange("p (b s) -> p b s", b=HALF),
                                        vo_bias[:, None, :].to_broadcast([P, HALF, D]), ALU.add).then_inc(vo_ready, 1)

            add_bias(0)
            dve.wait_ge(probs_turned, 1)
            nc.vector.tensor_copy(probsT[:, twos(0), :], bank[0][:, 0:256].rearrange("p (b s) -> p b s", b=2)).then_inc(probsT_ready, 1)
            add_bias(1)
            dve.wait_ge(probs_ready, B)
            nc.vector.reciprocal(inv_sum[:, :], row_sum[:, :]).then_inc(inv_ready, 1)
            dve.wait_ge(inv_ready, 1)
            for p in range(HALF - 1):
                dve.wait_ge(pv_done, p + 1)
                for b in (2 * p, 2 * p + 1):
                    nc.vector.scalar_tensor_tensor(x2[:, b, :], bank[PV_BANK[p]][:, (b % 2) * D:(b % 2 + 1) * D], inv_sum[:, b:b + 1],
                                                   x_sb[:, b, :], ALU.mult, ALU.add).then_inc(x2_ready, 1)
            for h in range(2):
                dve.wait_ge(x2_ready, min(HALF * (h + 1), B - 2))
                if h == 1:
                    dve.wait_ge(last_x2_ready, 1)
                moments(1, x2, h)
            dve.wait_ge(logits_done, 1)
            dve.wait_ge(rstd_ready, 4)
            nc.vector.tensor_tensor(logits[:, :, :], bank[2][:, 0:B * E].rearrange("p (b e) -> p b e", b=B),
                                    rstd[:, 1, :, None].to_broadcast([P, B, E]), ALU.mult).then_inc(logits_ready, 1)
            nc.vector.scalar_tensor_tensor(shift[:, :], mean_var[:, 1, :, 0], -1.0, rstd[:, 1, :], ALU.mult, ALU.mult)\
                .then_inc(shift_ready, 1)

            steps = [0]

            def step(ins):
                ins.then_inc(route_step, 1)
                steps[0] += 1
                dve.wait_ge(route_step, steps[0])

            dve.wait_ge(sigmoid_ready, 1)
            dve.wait_ge(rows_loaded, 16)
            step(nc.vector.tensor_tensor(sel[:, :, :], scores[:, :, :], ebias[:, None, :].to_broadcast([P, B, E]), ALU.add))
            for b in range(B):
                last = nc.vector.max(top_values[:, b, :], sel[:, b, :])
            step(last)
            for b in range(B):
                last = nc.vector.max_index(top_index[:, b, :], top_values[:, b, :], sel[:, b, :])
            step(last)
            dve.wait_ge(route_consts_ready, ROUTE_CONSTS)
            for k in range(TOP):
                nc.vector.tensor_tensor(onehot[:, :, k, :], expert_index[:, None, :].to_broadcast([P, B, E]),
                                        top_index[:, :, k:k + 1].to_broadcast([P, B, E]), ALU.is_equal).then_inc(onehot_ready, 1)

            def share(k):
                dve.wait_ge(silu_ready, k + 1)
                if k >= HJ:
                    dve.wait_ge(down_done, k - HJ + 1)
                nc.vector.tensor_tensor(hid[:, k % HJ, :], silu_t[:, k % 2, :], bank[5 + 2 * (k % 2)][:, :], ALU.mult)\
                    .then_inc(hid_ready, 1)

            def add_residual():
                dve.wait_ge(down_done, HJ)
                nc.vector.scalar_tensor_tensor(acc[:, :, :], bank[0][:, :].rearrange("p (b s) -> p b s", b=HALF), tanh_g[:, 1:2],
                                               x2[:, halves(0), :], ALU.mult, ALU.add).then_inc(acc_ready, 1)

            def slots():
                dve.wait_ge(counts_done, 1)
                nc.vector.tensor_scalar(padded_count[:, :], bank[2][0:RUNS, 128:129], ROUND, -ROUND, ALU.add, ALU.add)\
                    .then_inc(padded_ready, 1)
                dve.wait_ge(ranks_done, 1)
                dve.wait_ge(onehot_ready, 2)
                for k in range(TOP):
                    nc.vector.tensor_tensor(picked_rank[:, k * B:(k + 1) * B, :], onehot[:, :, k, :],
                                            bank[3][:, 0:B * RUNS].rearrange("p (b k e) -> p b k e", b=B, k=TOP)[:, :, k, :], ALU.mult)\
                        .then_inc(picked_rank_ready, 1)
                for k in range(TOP):
                    dve.wait_ge(picked_rank_ready, k + 1)
                    with nc.allow_low_precision(reason="whole numbers below 2^24"):
                        nc.vector.reduce_sum(slot[:, k * B:(k + 1) * B], picked_rank[:, k * B:(k + 1) * B, :], AX).then_inc(slot_ready, 1)
                share(0)
                dve.wait_ge(ends_done, 1)
                step(nc.vector.tensor_scalar(passed[:, :], bank[2][0:TILES, 256 + RUNS:256 + 2 * RUNS], tile_start[0:TILES, 0:1], None, ALU.is_le))
                step(nc.vector.reduce_sum(runs_before[:, :], passed[:, :], AX))
                step(nc.vector.tensor_scalar(tile_run[:, :], runs_before[:, :], float(RUNS - 1), None, ALU.min))
                step(nc.vector.tensor_scalar(second_set[:, :], tile_run[:, :], float(E), -float(E), ALU.is_ge, ALU.mult))
                nc.vector.tensor_tensor(tile_expert[:, :], tile_run[:, :], second_set[:, :], ALU.add).then_inc(tile_expert_ready, 1)
                nc.vector.tensor_scalar(tile_count[:, :], bank[2][0:1, 256 + 2 * RUNS - 1:256 + 2 * RUNS], 1.0 / P, None, ALU.mult)\
                    .then_inc(tile_expert_ready, 1)

            def make_gates():
                step(nc.vector.tensor_tensor(picked_score[:, :, :, :], onehot[:, :, :, :],
                                             scores[:, :, None, :].to_broadcast([P, B, TOP, E]), ALU.mult))
                step(nc.vector.reduce_sum(gate_raw[:, :], picked_score[:, :, :, :].rearrange("p b k e -> p (b k) e"), AX))
                nc.vector.tensor_scalar(gates[:, :], gate_raw[:, :], tanh_g[:, 1:2], None, ALU.mult).then_inc(gates_ready, 1)

            slots()
            for k in range(1, SHARED_EARLY):
                share(k)
                if k == 1:
                    make_gates()
                if k == HJ:
                    add_residual()

            dve.wait_ge(tile_expert_ready, 2)
            count = dve.value_load(tile_count[0:1, 0:1], min_val=GROUP * SURE, max_val=TILES)

            def evacuate(j):
                dve.wait_ge(r_down_done, j + 1)
                nc.vector.tensor_copy(tile_y[:, j, :], bank[j % 2][:, 0:D]).then_inc(tile_y_ready, 1)

            def group(g):
                for j in range(tiles(g).start, tiles(g).stop):
                    if j % PAIR == 0:
                        p = j // PAIR
                        dve.wait_ge(tile_x_loaded[p % ROWS_RING], 16 * (p // ROWS_RING + 1))
                        nc.vector.tensor_copy(tile_place[:, pair(p)], tile_x[:, pair(p), D]).then_inc(place_ready, 1)
                    i = j if j < EARLY else j - EARLY
                    if i == 1:
                        evacuate(j - 1)
                    dve.wait_ge(r_silu_ready, j + 1)
                    if j >= 3:
                        dve.wait_ge(r_down_done, j - 2)
                    nc.vector.tensor_tensor(tile_hid[:, j % 3, :], tile_silu[:, j % 2, :], bank[4 + j % UP_RING][:, P:2 * P], ALU.mult)\
                        .then_inc(r_hid_ready, 1)
                    if i > 2:
                        evacuate(j - 2)
                    if j == EARLY - 1:
                        evacuate(j - 1)
                        evacuate(j)

            def more_groups(g):
                if g < GROUPS:
                    with dve.If(count > GROUP * g):
                        group(g)
                        more_groups(g + 1)
                    with dve.Else():
                        evacuate(GROUP * g - 2)
                        evacuate(GROUP * g - 1)
                else:
                    evacuate(TILES - 2)
                    evacuate(TILES - 1)

            for g in range(SURE):
                group(g)
            more_groups(SURE)
            for k in range(SHARED_EARLY, 2 * HJ):
                share(k)
            dve.wait_ge(gates_ready, 1)
            for h, residual in enumerate((acc, x2)):
                dve.wait_ge(gated_ready, HALF * (h + 1))
                nc.vector.tensor_tensor(rest[:, halves(h), :], gated[:, halves(h), :], residual[:, halves(h), :], ALU.add)\
                    .then_inc(rest_ready, 1)
            dve.wait_ge(down_done, 2 * HJ)
            dve.wait_ge(rest_ready, 2)
            nc.vector.scalar_tensor_tensor(rest[:, halves(1), :], bank[1][:, :].rearrange("p (b s) -> p b s", b=HALF), tanh_g[:, 1:2],
                                           rest[:, halves(1), :], ALU.mult, ALU.add).then_inc(rest_ready, 1)
            for b in range(2, B):
                dve.wait_ge(rest_ready, 1 if b < HALF else 3)
                dve.wait_ge(y_loaded[b // 2], 16)
                nc.vector.scalar_tensor_tensor(final[:, b, :], picked_y[:, TOP * b + 1, :], gates[:, TOP * b + 1:TOP * b + 2],
                                               rest[:, b, :], ALU.mult, ALU.add).then_inc(last_final_ready, 1)

        @block.tensor
        def _(pe):
            def keep_warm(n, spare=7):
                for _ in range(n):
                    nc.tensor.transpose(bank[spare][:, 0:P], ident[:, :], ident[:, :])

            pe.wait_ge(ident_ready, 1)
            keep_warm(13)
            pe.wait_ge(params_loaded, 16)
            nc.tensor.transpose(bank[0][:, 0:128], wo_sb, ident[:, :]).then_inc(wo_turned, 1)
            nc.tensor.matmul(bank[1][:, 0:128], wq_sb, wk_sb, start=True, stop=True)
            nc.tensor.matmul(bank[1][:, 128:129], wk_sb, bq_col, start=True, stop=True).then_inc(fused_done, 1)
            pe.wait_ge(woT_ready, 1)
            nc.tensor.matmul(bank[6][:, 0:128], wv_sb, woT[:, :], start=True, stop=True).then_inc(fused_done, 1)

            def turn(dst, src, h, done):
                for b in range(HALF):
                    last = nc.tensor.transpose(dst[:, b * P:(b + 1) * P], src[:, HALF * h + b, :], ident[:, :])
                last.then_inc(done, 1)

            for h in range(2):
                pe.wait_ge(ctx_loaded[h], 16)
                turn(bank[2 + h], ctx_sb, h, ctx_turned)

            def turn_xn(h):
                pe.wait_ge(xn_ready, HALF * (h + 1))
                turn(bank[4 + h], xn, h, xn_turned)

            turn_xn(0)
            pe.wait_ge(bv_ready, 1)
            pe.wait_ge(rows_loaded, 16)
            pe.wait_ge(vo_w_ready, 1)
            nc.tensor.matmul(bank[6][:, 128:256], bv_mat[:, :], woT[:, :], start=True, stop=False)
            nc.tensor.matmul(bank[6][:, 128:256], ones_row[:, :], bo_row, start=False, stop=True).then_inc(fused_done, 1)
            nc.tensor.matmul(bank[7][:, 0:E], ones_mat[:, :], rw_sb, start=True, stop=True).then_inc(router_sum_done, 1)
            turn_xn(1)
            pe.wait_ge(fused_ready, 2)
            for h in range(2):
                pe.wait_ge(xnT_ready, h + 1)
                nc.tensor.matmul(bank[h][:, :], qk_w[:, :], xnT[:, halves(h), :], start=True, stop=True).then_inc(g_done, 1)
            for p in range(HALF):
                pe.wait_ge(g_ready, p // 2 + 1)
                pe.wait_ge(ctxT_ready, p // 2 + 1)
                for b in (2 * p, 2 * p + 1):
                    last = nc.tensor.matmul(bank[2 + p][:, (b % 2) * P:(b % 2 + 1) * P], gT[:, b, :], ctxT[:, b, :], start=True, stop=True)
                last.then_inc(scores_done, 1)

            def turn_probs(p):
                pe.wait_ge(probs_ready, 2 * p + 2)
                if p == 2:
                    pe.wait_ge(probsT_ready, 1)
                if p == 3:
                    pe.wait_ge(probsT_ready_too, 1)
                for b in (2 * p, 2 * p + 1):
                    last = nc.tensor.transpose(bank[p % 2][:, (b % 2) * P:(b % 2 + 1) * P], probs[:, b, :], ident[:, :])
                last.then_inc(probs_turned, 1)

            pe.wait_ge(bias_ready, 1)
            for h in range(2):
                if h == 1:
                    pe.wait_ge(router_ready, 1)
                for b in range(HALF):
                    last = nc.tensor.matmul(bank[6 + h][:, b * P:(b + 1) * P], ctxT[:, HALF * h + b, :], vo_w[:, :], start=True, stop=True)
                last.then_inc(vo_done, 1)
                if h == 0:
                    turn_probs(0)

            def attend(p):
                if p == 0:
                    pe.wait_ge(probsT_ready, 1)
                else:
                    pe.wait_ge(probsT_ready_too, p)
                pe.wait_ge(vo_ready, p // 2 + 1)
                for b in (2 * p, 2 * p + 1):
                    last = nc.tensor.matmul(bank[PV_BANK[p]][:, (b % 2) * P:(b % 2 + 1) * P], probsT[:, b, :], vo[:, b, :], start=True, stop=True)
                last.then_inc(pv_done, 1)

            turn_probs(1)
            turn_probs(2)
            attend(0)
            turn_probs(3)
            attend(1)
            attend(2)
            attend(3)
            for h in range(2):
                pe.wait_ge(x2_ready, min(HALF * (h + 1), B - 2))
                if h == 1:
                    pe.wait_ge(last_x2_ready, 1)
                turn(bank[4 + h], x2, h, x2_turned)
                keep_warm(3, 1)
            for h in range(2):
                pe.wait_ge(x2T_ready, h + 1)
                for b in range(HALF):
                    k = HALF * h + b
                    last = nc.tensor.matmul(bank[2][:, k * E:(k + 1) * E], x2T[:, k, :], router_c[:, :], start=True, stop=True)
            last.then_inc(logits_done, 1)
            keep_warm(22, 3)
            pe.wait_ge(x2n_ready, HALF)
            turn(bank[0], x2n[:, 0, :, 0:D], 0, x2n_turned)
            keep_warm(3, 1)

            def count_rows():
                pe.wait_ge(onehot_ready, 2)
                for b in range(B):
                    nc.tensor.matmul(bank[2][0:RUNS, 128:129], onehot[:, b, :, :].rearrange("p k e -> p (k e)"), ones_bf[:, 0:1],
                                     start=(b == 0), stop=False)
                last = nc.tensor.matmul(bank[2][0:RUNS, 128:129], half_less[:, :], ones_bf[0:1, 0:1], start=False, stop=True)
                last.then_inc(counts_done, 1)
                nc.tensor.matmul(bank[3][:, 0:B * RUNS], earlier_token[:, :], onehot[:, :, :, :].rearrange("p b k e -> p (b k e)"),
                                 start=True, stop=False, skip_group_check=True)
                for b in range(B - 1):
                    nc.tensor.matmul(bank[3][:, (b + 1) * RUNS:B * RUNS], ones_bf[:, :],
                                     onehot[:, b:b + 1, :, :].rearrange("p b k e -> p b (k e)").to_broadcast([P, B - 1 - b, RUNS]),
                                     start=False, stop=False, skip_group_check=True)

            def rank_rows():
                pe.wait_ge(padded_ready, 1)
                first_slots = padded_count[:, 0:1].to_broadcast([RUNS, P])
                nc.tensor.matmul(bank[3][:, 0:B * RUNS].rearrange("p (b r) -> p b r", b=B), first_slots,
                                 run_order[:, 0:1, :].to_broadcast([RUNS, B, RUNS]), start=False, stop=True, skip_group_check=True)\
                    .then_inc(ranks_done, 1)
                nc.tensor.matmul(bank[2][:, 256:256 + 2 * RUNS], first_slots, run_order[:, :, :].rearrange("p a r -> p (a r)"),
                                 start=True, stop=True).then_inc(ends_done, 1)

            count_rows()
            keep_warm(1, 1)
            rank_rows()

            def share_up(k):
                t, j = k // HJ, k % HJ
                if k >= 2:
                    pe.wait_ge(hid_ready, k - 1)
                a = bank[4 + 2 * (k % 2)]
                u = bank[5 + 2 * (k % 2)]
                xt = x2nT[:, halves(t), :]
                pe.wait_ge(x2nT_ready, t + 1)
                nc.tensor.matmul(a[:, :], w1s[:, j * P:(j + 1) * P], xt, start=True, stop=True)
                nc.tensor.matmul(u[:, :], w2s[:, j * P:(j + 1) * P], xt, start=True, stop=True).then_inc(up_done, 1)

            def share_down(k):
                t, j = k // HJ, k % HJ
                pe.wait_ge(hid_ready, k + 1)
                for b in range(HALF):
                    last = nc.tensor.matmul(bank[t][:, b * P:(b + 1) * P], hid[:, j, b * P:(b + 1) * P], w3s[:, j, :],
                                            start=(j == 0 and b == 0), stop=(j == HJ - 1), skip_group_check=True)
                last.then_inc(down_done, 1)

            pe.wait_ge(shared_loaded, 16)
            for k in range(SHARED_EARLY):
                share_up(k)
                if k == 0:
                    pe.wait_ge(x2n_ready, B)
                    turn(bank[1], x2n[:, 0, :, 0:D], 1, x2n_turned)
                if 2 <= k < HJ + 2:
                    share_down(k - 2)
            pe.wait_ge(tile_expert_ready, 2)
            count = pe.value_load(tile_count[0:1, 0:1], min_val=GROUP * SURE, max_val=TILES)

            def turn_tiles(p):
                pe.wait_ge(tile_x_loaded[p % ROWS_RING], 16 * (p // ROWS_RING + 1))
                if p >= 2:
                    pe.wait_ge(tile_xT_ready, p - 1)
                for i in range(tiles_in_pair(p)):
                    last = nc.tensor.transpose(bank[2 + p % 2][:, i * P:(i + 1) * P], tile_x[:, PAIR * p + i, 0:D], ident[:, :])
                last.then_inc(tile_turned, 1)

            def up(j):
                pe.wait_ge(tile_w_loaded[j % WEIGHT_RING], 16 * (j // WEIGHT_RING + 1))
                pe.wait_ge(tile_xT_ready, j // PAIR + 1)
                if j >= UP_RING:
                    pe.wait_ge(r_hid_ready, j - UP_RING + 1)
                xt = tile_xT[:, j // PAIR % 3, (j % PAIR) * P:(j % PAIR + 1) * P]
                dst = bank[4 + j % UP_RING]
                nc.tensor.matmul(dst[:, 0:P], tile_w[:, j % WEIGHT_RING, 0:P], xt, start=True, stop=True)
                nc.tensor.matmul(dst[:, P:2 * P], tile_w[:, j % WEIGHT_RING, P:2 * P], xt, start=True, stop=True).then_inc(r_up_done, 1)

            def down(j):
                pe.wait_ge(r_hid_ready, j + 1)
                if j >= 2:
                    pe.wait_ge(tile_y_ready, j - 1)
                nc.tensor.matmul(bank[j % 2][:, 0:D], tile_hid[:, j % 3, :], tile_w[:, j % WEIGHT_RING, 2 * P:3 * P], start=True, stop=True)\
                    .then_inc(r_down_done, 1)

            def group(g):
                for j in range(tiles(g).start, tiles(g).stop):
                    i = j if j < EARLY else j - EARLY
                    if i == 0:
                        turn_tiles(j // PAIR)
                    if j in (0, 2):
                        pe.wait_ge(hid_ready, SHARED_EARLY - 1 + j // 2)
                    up(j)
                    if j % PAIR == 0 and j + PAIR not in (EARLY, TILES):
                        turn_tiles(j // PAIR + 1)
                    if i == 1:
                        if j == 1:
                            pe.wait_ge(acc_ready, 1)
                        down(j - 1)
                    elif i > 2:
                        down(j - 2)
                    if j == EARLY - 1:
                        down(j - 1)
                        down(j)

            def more_groups(g):
                if g < GROUPS:
                    with pe.If(count > GROUP * g):
                        group(g)
                        more_groups(g + 1)
                    with pe.Else():
                        down(GROUP * g - 2)
                        down(GROUP * g - 1)
                else:
                    down(TILES - 2)
                    down(TILES - 1)

            for g in range(SURE):
                group(g)
            more_groups(SURE)
            for k in range(SHARED_EARLY, 2 * HJ):
                share_up(k)
            for k in range(HJ, 2 * HJ):
                pe.wait_ge(hid_ready, 2 * HJ - 1)
                share_down(k)


_INS = ['x', 'ctx_1024']


def kernel(**inputs):
    import numpy as _np
    import concourse.bacc as _bacc
    from concourse import mybir as _mybir
    from concourse.bass_utils import run_bass_kernel_spmd as _run

    nc = _bacc.Bacc("TRN2", target_bir_lowering=False, num_devices=1)
    arrays, args = {}, []
    for name in _INS:
        a = _np.ascontiguousarray(inputs[name])
        arrays[f"in_{name}_dram"] = a
        args.append(nc.dram_tensor(f"in_{name}_dram", a.shape, _mybir.dt.from_np(a.dtype), kind="ExternalInput").ap())
    w = {k.split("_", 1)[-1]: _np.asarray(v) for k, v in inputs.items()}
    s3 = w["ffn_shared_w3"][0]
    d = s3.shape[1]
    packed = {
        "attn_params": _np.concatenate([w["xattn_Wo"], w["xattn_Wq"], w["xattn_Wk"], w["xattn_Wv"], w["xattn_bq"][:, None],
                                        w["xattn_bv"][:, None], w["ffn_router_w"]], axis=1),
        "row_params": _np.concatenate([w["xattn_bo"], w["ffn_expert_bias"], _np.asarray(inputs["g_xattn"]),
                                       _np.asarray(inputs["g_ffn"])])[None, :],
        "shared_w": _np.concatenate([w["ffn_shared_w1"][0], w["ffn_shared_w2"][0],
                                     s3.reshape(-1, d, d).transpose(1, 0, 2).reshape(d, -1)], axis=1),
        "routed_w": _np.concatenate([w["ffn_routed_w1"], w["ffn_routed_w2"], w["ffn_routed_w3"]], axis=2),
    }
    for name, a in packed.items():
        arrays[f"in_{name}_dram"] = a
        args.append(nc.dram_tensor(f"in_{name}_dram", a.shape, _mybir.dt.from_np(a.dtype), kind="ExternalInput").ap())
    shape = inputs["x"].shape
    args.append(nc.dram_tensor("out_0_dram", shape, _mybir.dt.float32, kind="ExternalOutput").ap())
    flamingo_block(nc, *args)
    r = _run(nc, [arrays], core_ids=[0])
    return r.results[0]["out_0_dram"]
```
